# Optimizing a Trainium2 kernel written in Bass

```python
import numpy as np
import jax
import jax.numpy as jnp

def _softmax(x, axis=-1):
    return jax.nn.softmax(x, axis=axis)

def _gelu(x):
    return jax.nn.gelu(x, approximate=True)

def _silu(x):
    return jax.nn.silu(x)

def _sigmoid(x):
    return jax.nn.sigmoid(x)

def _layernorm(x, axis=-1, eps=1e-05):
    m = jnp.mean(x, axis=axis, keepdims=True)
    v = jnp.var(x, axis=axis, keepdims=True)
    return (x - m) / jnp.sqrt(v + eps)

def _scatter_add(tgt, idx, src, axis=0):
    return tgt.at[idx].add(src)

def _segment_sum(src, seg, n):
    return jax.ops.segment_sum(src, seg, n)
kernel_name = 'mk_perceiver_d1_seqx_r8_6532a8'

def setup_inputs(seed: int=0):
    np.random.seed(seed)
    _w = jnp.asarray

    def _rec_inputs():
        import jax
        import jax.numpy as jnp
        _rk = jax.random.key(seed)
        x = 7.22e-05 + 1 * jax.random.normal(jax.random.fold_in(_rk, 1), (1, 64, 128), jnp.float32)
        _lenS = 64 - jax.random.randint(jax.random.fold_in(_rk, 7), (1,), 0, max(1, 64 // 4) + 1, jnp.int32)
        _lenS2 = 6272 - jax.random.randint(jax.random.fold_in(_rk, 8), (1,), 0, max(1, 6272 // 4) + 1, jnp.int32)
        _ctx_1024P = jax.random.normal(jax.random.fold_in(_rk, 11), (1, 16, 128), jnp.float32)
        _ctx_1024c = jax.random.dirichlet(jax.random.fold_in(_rk, 511), 0.3 * jnp.ones((16,), jnp.float32), (1, 6272))
        _ctx_1024t = jnp.einsum('bsk,bkd->bsd', _ctx_1024c, _ctx_1024P)
        _ctx_1024t = _ctx_1024t * jax.lax.rsqrt(jnp.mean(jnp.square(_ctx_1024t)) + 1e-12) * 0.953939
        ctx_1024 = 4.13588e-05 + 0.999923 * (_ctx_1024t + 0.3 * jax.random.normal(jax.random.fold_in(_rk, 611), (1, 6272, 128), jnp.float32))
        return (x, ctx_1024)
    x, ctx_1024 = _rec_inputs()

    def _L0_xattn_setup():
        import jax, jax.numpy as jnp
        import numpy as np
        DIM = 128
        HEADS = 16
        DIM_HEAD = 64
        INNER = HEADS * DIM_HEAD
        MLP = 512
        EPS = 1e-05

        def _layernorm(x, g, b):
            mu = jnp.mean(x, axis=-1, keepdims=True)
            var = jnp.mean(jnp.square(x - mu), axis=-1, keepdims=True)
            return (x - mu) * jax.lax.rsqrt(var + EPS) * g + b

        def _l2norm(x):
            n = jnp.sqrt(jnp.sum(jnp.square(x), axis=-1, keepdims=True))
            return x / jnp.maximum(n, 1e-12)

        def _split_heads(x, B, N):
            return x.reshape(B, N, HEADS, DIM_HEAD).transpose(0, 2, 1, 3)
        key = jax.random.key(seed)
        ks = jax.random.split(key, 16)
        B, N = (4, 256)
        s = 0.02
        return {'Q': jax.random.normal(ks[0], (B, N, DIM), jnp.float32), 'K': jax.random.normal(ks[1], (B, N, DIM), jnp.float32), 'V': jax.random.normal(ks[2], (B, N, DIM), jnp.float32), 'wq': jax.random.normal(ks[3], (DIM, INNER), jnp.float32) * s, 'wk': jax.random.normal(ks[4], (DIM, INNER), jnp.float32) * s, 'wv': jax.random.normal(ks[5], (DIM, INNER), jnp.float32) * s, 'wo': jax.random.normal(ks[6], (INNER, DIM), jnp.float32) * s, 'bo': jnp.zeros((DIM,), jnp.float32), 'w1': jax.random.normal(ks[7], (DIM, MLP), jnp.float32) * s, 'b1': jnp.zeros((MLP,), jnp.float32), 'w2': jax.random.normal(ks[8], (MLP, DIM), jnp.float32) * s, 'b2': jnp.zeros((DIM,), jnp.float32), 'ln1_g': jnp.ones((DIM,), jnp.float32), 'ln1_b': jnp.zeros((DIM,), jnp.float32), 'ln2_g': jnp.ones((DIM,), jnp.float32), 'ln2_b': jnp.zeros((DIM,), jnp.float32)}
    _L0_xattn_all = _L0_xattn_setup()
    _L0_xattn_in = {k: v for k, v in _L0_xattn_all.items() if k in ('wq', 'wk', 'wv', 'wo', 'bo', 'w1', 'b1', 'w2', 'b2', 'ln1_g', 'ln1_b', 'ln2_g', 'ln2_b')}
    del _L0_xattn_all

    def _L0_attn_setup():
        import jax, jax.numpy as jnp
        import numpy as np
        D_MODEL = 128
        NUM_HEADS = 16
        HEAD_DIM = D_MODEL // NUM_HEADS
        key = jax.random.key(seed)
        ks = jax.random.split(key, 10)
        B, L = (2, 256)
        s = 1.0 / np.sqrt(D_MODEL)
        x = jax.random.normal(ks[0], (B, L, D_MODEL), dtype=jnp.float32)
        Wq = jax.random.normal(ks[1], (D_MODEL, D_MODEL), dtype=jnp.float32) * s
        bq = jnp.zeros((D_MODEL,), dtype=jnp.float32)
        Wk = jax.random.normal(ks[2], (D_MODEL, D_MODEL), dtype=jnp.float32) * s
        bk = jnp.zeros((D_MODEL,), dtype=jnp.float32)
        Wv = jax.random.normal(ks[3], (D_MODEL, D_MODEL), dtype=jnp.float32) * s
        bv = jnp.zeros((D_MODEL,), dtype=jnp.float32)
        Wo = jax.random.normal(ks[4], (D_MODEL, D_MODEL), dtype=jnp.float32) * s
        bo = jnp.zeros((D_MODEL,), dtype=jnp.float32)
        gamma = jax.random.uniform(ks[5], (NUM_HEADS,), dtype=jnp.float32, minval=0.95, maxval=1.0)
        return {'x': x, 'Wq': Wq, 'bq': bq, 'Wk': Wk, 'bk': bk, 'Wv': Wv, 'bv': bv, 'Wo': Wo, 'bo': bo, 'gamma': gamma}
    _L0_attn_all = _L0_attn_setup()
    _L0_attn_in = {k: v for k, v in _L0_attn_all.items() if k in ('Wq', 'bq', 'Wk', 'bk', 'Wv', 'bv', 'Wo', 'bo', 'gamma')}
    del _L0_attn_all

    def _L0_ffn_setup():
        import jax, jax.numpy as jnp
        import numpy as np
        B, S, H, F, G = (8, 256, 128, 512, 128)
        EPS = 1e-05

        def _dequant(q, scales, g):
            K, N = q.shape
            w = (q.astype(jnp.float32) - 128.0).reshape(K // g, g, N) * scales[:, None, :]
            return w.reshape(K, N)
        key = jax.random.key(seed)
        ks = jax.random.split(key, 8)
        x = jax.random.normal(ks[0], (B, S, H), dtype=jnp.float32)
        ln_gamma = jnp.ones((H,), jnp.float32)
        ln_beta = jnp.zeros((H,), jnp.float32)
        fc1_q = jax.random.randint(ks[1], (H, F), 0, 32, dtype=jnp.int32)
        fc2_q = jax.random.randint(ks[2], (F, H), 0, 32, dtype=jnp.int32)
        fc1_scales = jax.random.uniform(ks[3], (H // G, F), jnp.float32) * 0.02 + 0.001
        fc2_scales = jax.random.uniform(ks[4], (F // G, H), jnp.float32) * 0.02 + 0.001
        fc1_bias = jax.random.normal(ks[5], (F,), jnp.float32) * 0.02
        fc2_bias = jax.random.normal(ks[6], (H,), jnp.float32) * 0.02
        return {'x': x, 'ln_gamma': ln_gamma, 'ln_beta': ln_beta, 'fc1_q': fc1_q, 'fc1_scales': fc1_scales, 'fc1_bias': fc1_bias, 'fc2_q': fc2_q, 'fc2_scales': fc2_scales, 'fc2_bias': fc2_bias}
    _L0_ffn_all = _L0_ffn_setup()
    _L0_ffn_in = {k: v for k, v in _L0_ffn_all.items() if k in ('ln_gamma', 'ln_beta', 'fc1_q', 'fc1_scales', 'fc1_bias', 'fc2_q', 'fc2_scales', 'fc2_bias')}
    del _L0_ffn_all
    return {'x': x, 'ctx_1024': ctx_1024, 'L0_xattn_wq': _L0_xattn_in['wq'], 'L0_xattn_wk': _L0_xattn_in['wk'], 'L0_xattn_wv': _L0_xattn_in['wv'], 'L0_xattn_wo': _L0_xattn_in['wo'], 'L0_xattn_bo': _L0_xattn_in['bo'], 'L0_xattn_w1': _L0_xattn_in['w1'], 'L0_xattn_b1': _L0_xattn_in['b1'], 'L0_xattn_w2': _L0_xattn_in['w2'], 'L0_xattn_b2': _L0_xattn_in['b2'], 'L0_xattn_ln1_g': _L0_xattn_in['ln1_g'], 'L0_xattn_ln1_b': _L0_xattn_in['ln1_b'], 'L0_xattn_ln2_g': _L0_xattn_in['ln2_g'], 'L0_xattn_ln2_b': _L0_xattn_in['ln2_b'], 'L0_attn_Wq': _L0_attn_in['Wq'], 'L0_attn_bq': _L0_attn_in['bq'], 'L0_attn_Wk': _L0_attn_in['Wk'], 'L0_attn_bk': _L0_attn_in['bk'], 'L0_attn_Wv': _L0_attn_in['Wv'], 'L0_attn_bv': _L0_attn_in['bv'], 'L0_attn_Wo': _L0_attn_in['Wo'], 'L0_attn_bo': _L0_attn_in['bo'], 'L0_attn_gamma': _L0_attn_in['gamma'], 'L0_ffn_ln_gamma': _L0_ffn_in['ln_gamma'], 'L0_ffn_ln_beta': _L0_ffn_in['ln_beta'], 'L0_ffn_fc1_q': _L0_ffn_in['fc1_q'], 'L0_ffn_fc1_scales': _L0_ffn_in['fc1_scales'], 'L0_ffn_fc1_bias': _L0_ffn_in['fc1_bias'], 'L0_ffn_fc2_q': _L0_ffn_in['fc2_q'], 'L0_ffn_fc2_scales': _L0_ffn_in['fc2_scales'], 'L0_ffn_fc2_bias': _L0_ffn_in['fc2_bias']}

def reference(x, ctx_1024, L0_xattn_wq, L0_xattn_wk, L0_xattn_wv, L0_xattn_wo, L0_xattn_bo, L0_xattn_w1, L0_xattn_b1, L0_xattn_w2, L0_xattn_b2, L0_xattn_ln1_g, L0_xattn_ln1_b, L0_xattn_ln2_g, L0_xattn_ln2_b, L0_attn_Wq, L0_attn_bq, L0_attn_Wk, L0_attn_bk, L0_attn_Wv, L0_attn_bv, L0_attn_Wo, L0_attn_bo, L0_attn_gamma, L0_ffn_ln_gamma, L0_ffn_ln_beta, L0_ffn_fc1_q, L0_ffn_fc1_scales, L0_ffn_fc1_bias, L0_ffn_fc2_q, L0_ffn_fc2_scales, L0_ffn_fc2_bias):
    import jax
    import jax.numpy as jnp

    def _L0_xattn_ref(Q, K, V, wq, wk, wv, wo, bo, w1, b1, w2, b2, ln1_g, ln1_b, ln2_g, ln2_b):
        import jax, jax.numpy as jnp
        import numpy as np
        DIM = 128
        HEADS = 16
        DIM_HEAD = 64
        INNER = HEADS * DIM_HEAD
        MLP = 512
        EPS = 1e-05

        def _layernorm(x, g, b):
            mu = jnp.mean(x, axis=-1, keepdims=True)
            var = jnp.mean(jnp.square(x - mu), axis=-1, keepdims=True)
            return (x - mu) * jax.lax.rsqrt(var + EPS) * g + b

        def _l2norm(x):
            n = jnp.sqrt(jnp.sum(jnp.square(x), axis=-1, keepdims=True))
            return x / jnp.maximum(n, 1e-12)

        def _split_heads(x, B, N):
            return x.reshape(B, N, HEADS, DIM_HEAD).transpose(0, 2, 1, 3)
        B, Nq, _ = Q.shape
        Nk = K.shape[1]
        Qn = _layernorm(Q, ln1_g, ln1_b)
        Kn = _layernorm(K, ln1_g, ln1_b)
        Vn = _layernorm(V, ln1_g, ln1_b)
        q = _split_heads(Qn @ wq, B, Nq)
        k = _split_heads(Kn @ wk, B, Nk)
        v = _split_heads(Vn @ wv, B, Nk)
        qn = _l2norm(q)
        kn = _l2norm(k)
        attn = jnp.einsum('bhqd,bhkd->bhqk', qn, kn)
        out = jnp.einsum('bhqk,bhkd->bhqd', attn, v)
        out = out.transpose(0, 2, 1, 3).reshape(B, Nq, INNER)
        x = Q + out @ wo + bo
        xn = _layernorm(x, ln2_g, ln2_b)
        h = jax.nn.gelu(xn @ w1 + b1, approximate=False)
        return x + h @ w2 + b2

    def _L0_attn_ref(x, Wq, bq, Wk, bk, Wv, bv, Wo, bo, gamma):
        import jax, jax.numpy as jnp
        import numpy as np
        D_MODEL = 128
        NUM_HEADS = 16
        HEAD_DIM = D_MODEL // NUM_HEADS
        B, L, D = x.shape
        H, hd = (NUM_HEADS, HEAD_DIM)
        q = (x @ Wq.T + bq).reshape(B, L, H, hd).transpose(0, 2, 1, 3)
        k = (x @ Wk.T + bk).reshape(B, L, H, hd).transpose(0, 2, 1, 3)
        v = (x @ Wv.T + bv).reshape(B, L, H, hd).transpose(0, 2, 1, 3)
        idx = jnp.arange(L, dtype=x.dtype)
        decay = gamma[None, :, None, None] ** idx[None, None, :, None]
        scores = jnp.einsum('bhqd,bhkd->bhqk', q, k)
        causal = jnp.tril(jnp.ones((L, L), dtype=x.dtype))
        scores = scores * causal[None, None] * decay
        out = jnp.einsum('bhqk,bhkd->bhqd', scores, v)
        out = out.transpose(0, 2, 1, 3).reshape(B, L, D)
        return out @ Wo.T + bo

    def _L0_ffn_ref(x, ln_gamma, ln_beta, fc1_q, fc1_scales, fc1_bias, fc2_q, fc2_scales, fc2_bias):
        import jax, jax.numpy as jnp
        import numpy as np
        B, S, H, F, G = (8, 256, 128, 512, 128)
        EPS = 1e-05

        def _dequant(q, scales, g):
            K, N = q.shape
            w = (q.astype(jnp.float32) - 128.0).reshape(K // g, g, N) * scales[:, None, :]
            return w.reshape(K, N)
        residual = x
        mu = jnp.mean(x, axis=-1, keepdims=True)
        var = jnp.mean(jnp.square(x - mu), axis=-1, keepdims=True)
        h = (x - mu) * jax.lax.rsqrt(var + EPS) * ln_gamma + ln_beta
        hf = h.reshape(-1, H)
        w1 = _dequant(fc1_q, fc1_scales, G)
        y = hf @ w1 + fc1_bias
        y = jax.nn.silu(y)
        w2 = _dequant(fc2_q, fc2_scales, G)
        z = y @ w2 + fc2_bias
        return residual + 0.5 * z.reshape(residual.shape)
    x = x + _L0_xattn_ref(_layernorm(x, axis=-1), ctx_1024, ctx_1024, L0_xattn_wq, L0_xattn_wk, L0_xattn_wv, L0_xattn_wo, L0_xattn_bo, L0_xattn_w1, L0_xattn_b1, L0_xattn_w2, L0_xattn_b2, L0_xattn_ln1_g, L0_xattn_ln1_b, L0_xattn_ln2_g, L0_xattn_ln2_b)
    x = x + _L0_attn_ref(_layernorm(x, axis=-1), L0_attn_Wq, L0_attn_bq, L0_attn_Wk, L0_attn_bk, L0_attn_Wv, L0_attn_bv, L0_attn_Wo, L0_attn_bo, L0_attn_gamma)
    x = x + _L0_ffn_ref(_layernorm(x, axis=-1), L0_ffn_ln_gamma, L0_ffn_ln_beta, L0_ffn_fc1_q, L0_ffn_fc1_scales, L0_ffn_fc1_bias, L0_ffn_fc2_q, L0_ffn_fc2_scales, L0_ffn_fc2_bias)
    return x

_drawn_inputs = setup_inputs


def setup_inputs(seed=0):
    import zlib

    import numpy as np

    out = dict(_drawn_inputs(seed))
    spreads = {'L0_xattn_bo': (0.0, 2.0),
     'L0_xattn_b1': (0.0, 0.8),
     'L0_xattn_b2': (0.0, 0.8),
     'L0_xattn_ln1_g': (1.0, 0.2),
     'L0_xattn_ln1_b': (0.0, 0.1),
     'L0_xattn_ln2_g': (1.0, 0.6),
     'L0_xattn_ln2_b': (0.0, 0.8),
     'L0_attn_bq': (0.0, 0.1),
     'L0_attn_bk': (0.0, 0.286),
     'L0_attn_bv': (0.0, 0.481),
     'L0_attn_bo': (0.0, 2.0),
     'L0_ffn_ln_gamma': (1.0, 0.2),
     'L0_ffn_ln_beta': (0.0, 0.1)}
    factors = {'L0_xattn_w1': 8.0,
     'L0_xattn_w2': 8.0,
     'L0_ffn_fc1_scales': 10.334,
     'L0_ffn_fc1_bias': 64.0,
     'L0_ffn_fc2_bias': 64.0}
    for name, (base, spread) in spreads.items():
        noise = np.random.default_rng([zlib.crc32(name.encode()), seed]).standard_normal(out[name].shape)
        drawn = base * np.exp(spread * noise) if base else spread * noise
        out[name] = jnp.asarray(drawn.astype(out[name].dtype))
    for name, factor in factors.items():
        out[name] = (out[name] * factor).astype(out[name].dtype)
    return out
```

```python
from contextlib import ExitStack

import concourse.bass as bass
from concourse import mybir

F32 = mybir.dt.float32
F32R = mybir.dt.float32r
I32 = mybir.dt.int32
ALU = mybir.AluOpType
ACT = mybir.ActivationFunctionType
AX_X = mybir.AxisListType.X

P = 128
D = 128
TOK = 64
CTX = 6272
TILES = CTX // P
GROUP = 4
BODY = 8
ITERS = (TILES - 1) // BODY
XH, XD = 16, 64
INNER = XH * XD
PAIRS = INNER // P
HALF = INNER // 2
MLP = 512
MC = MLP // P
AH, AD = 16, 8
ROWG = 4
EPS = 1e-5
TINY = 1e-12
KN = 4

COLS = ["ln1_g", "ln1_b", "ln2_g", "ln2_b", "fln_g", "fln_b", "bq", "bk", "b1", "fc1_b"]
CW = 8 + 2 * MC
R_BO, R_B2, R_ABO, R_FB2, R_BV, R_GAM, R_S1, R_S2 = 0, 128, 256, 384, 512, 640, 656, 1168
RW = 1680
C_ID, C_CAUSAL, C_HEAD, C_GRP, C_IDX = 0, 128, 192, 196, 200
CCW = 216


def build_kernel(nc, x, ctx_rows, wq, wk, wv, wo, w1, w2, wqT, wkT, wvT, woT, fc1, fc2, cols, rows, consts,
                 chunk_select, out):
    ctx = ExitStack()
    with ctx:
        def sb(name, shape, dt=F32):
            return ctx.enter_context(nc.sbuf_tensor(name, shape, dt))

        def sem(name):
            return ctx.enter_context(nc.semaphore(name))

        cst = sb("cst", [P, CCW])
        col = sb("col", [P, CW])
        row = sb("row", [P, RW])
        sel = sb("sel", [2 * MC, 2 * MC * TOK])
        xs = sb("xs", [TOK, D])
        wq_s = sb("wq_s", [P, INNER])
        wk_s = sb("wk_s", [P, INNER])
        wv_s = sb("wv_s", [P, INNER])
        wo_s = sb("wo_s", [P, PAIRS, D])
        w1_s = sb("w1_s", [P, MLP])
        w2_s = sb("w2_s", [P, MC, D])
        attn_w = sb("attn_w", [P, 4, D])
        fc1_q = sb("fc1_q", [P, MLP], I32)
        fc2_q = sb("fc2_q", [P, MC, D], I32)
        ident = cst[:, C_ID:C_ID + P]
        ctx_s = sb("ctx_s", [P, 3, GROUP, D])
        z = sb("z", [P, 3, GROUP, D])
        zT_hi = sb("zT_hi", [P, 3, GROUP * P], F32R)
        zT_lo = sb("zT_lo", [P, 3, GROUP * P], F32R)
        bn = sb("bn", [P, 3, GROUP, 6])
        mv = sb("mv", [P, 3, GROUP, 2])
        ln_std = sb("ln_std", [P, 3, GROUP])
        ln_r = sb("ln_r", [P, 3, GROUP])
        ln_mr = sb("ln_mr", [P, 3, GROUP])
        ln_c = sb("ln_c", [P, 3, GROUP])
        k_sq = sb("k_sq", [P, 2, INNER])
        n2 = sb("n2", [P, KN, XH])
        nrm = sb("nrm", [P, KN, XH])
        nrm_floor = sb("nrm_floor", [P, KN, XH])
        rinv = sb("rinv", [P, KN, XH])
        kn = sb("kn", [P, KN, INNER])
        fold_d = sb("fold_d", [P, 2])
        fold = sb("fold", [P, P])
        wk_hi = sb("wk_hi", [P, INNER], F32R)
        wk_lo = sb("wk_lo", [P, INNER], F32R)
        wv_f = sb("wv_f", [P, INNER])
        x_bn = sb("x_bn", [TOK, 6])
        x_mv = sb("x_mv", [TOK, 2])
        x_std = sb("x_std", [TOK, 2])
        x_r = sb("x_r", [TOK, 2])
        xl = sb("xl", [TOK, D])
        xl_bo = sb("xl_bo", [TOK, D])
        x_b2 = sb("x_b2", [TOK, D])
        xq = sb("xq", [TOK, D])
        xqT = sb("xqT", [P, TOK])
        q_sq = sb("q_sq", [TOK, INNER])
        q_n2 = sb("q_n2", [TOK, 4, XH])
        qn = sb("qn", [TOK, INNER])
        qnT = sb("qnT", [P, PAIRS, TOK])
        w1_g = sb("w1_g", [P, MLP])
        fc1_d = sb("fc1_d", [P, MLP])
        fc1_f = sb("fc1_f", [P, MLP])
        fc1_g = sb("fc1_g", [P, MLP])
        fc2_f = sb("fc2_f", [P, MC, D])
        fc2_d = sb("fc2_d", [P, MC, D])
        bias_c = sb("bias_c", [P, 2 * MC])
        biasT = sb("biasT", [2 * MC, P])
        decay = sb("decay", [TOK, AH])
        half_neg = sb("half_neg", [TOK, 2])
        warm = sb("warm", [TOK, 2])
        eps_tile = sb("eps_tile", [P, 2])
        ones_row = sb("ones_row", [1, P])
        gT = sb("gT", [P, INNER])
        m_bd = sb("m_bd", [P, PAIRS, P])
        oT = sb("oT", [P, PAIRS, TOK])
        x1 = sb("x1", [TOK, D])
        x1_r = sb("x1_r", [TOK, D])
        t_bn = sb("t_bn", [TOK, 3, 6])
        t_mv = sb("t_mv", [TOK, 3, 2])
        t_ve = sb("t_ve", [TOK, 3, 2])
        t_r = sb("t_r", [TOK, 3, 2])
        t_hat = sb("t_hat", [TOK, 3, D])
        hatT = sb("hatT", [P, 3, P])
        h1 = sb("h1", [P, MC * TOK])
        x2 = sb("x2", [TOK, D])
        x2_r = sb("x2_r", [TOK, D])
        q_heads = sb("q_heads", [P, ROWG, TOK])
        k_groups = sb("k_groups", [P, ROWG, TOK])
        v_s = sb("v_s", [P, D])
        scores = sb("scores", [P, 8, TOK])
        a_out = sb("a_out", [TOK, D])
        a_outT = sb("a_outT", [P, TOK])
        x3 = sb("x3", [TOK, D])
        u = sb("u", [TOK, D])
        x3_u = sb("x3_u", [TOK, D])
        fb_half = sb("fb_half", [TOK, D])
        x3_r = sb("x3_r", [TOK, D])
        h2 = sb("h2", [P, MC * TOK])
        y_out = sb("y_out", [TOK, D])
        ps = ctx.enter_context(nc.psum_tensor("ps", [P, 8, 512], F32))
        g_ps = ps[:, 0:2, :]
        k_ps = [ps[:, 2:4, :], ps[:, 4:6, :]]
        zT_ps = ps[:, 6, :]
        misc = ps[:, 7, :]

        in_small = sem("in_small")
        in_x = sem("in_x")
        in_wk = sem("in_wk")
        in_wq = sem("in_wq")
        in_wv = sem("in_wv")
        in_row = sem("in_row")
        in_pool_w = sem("in_pool_w")
        in_tail_w = sem("in_tail_w")
        ctx_in = [sem("ctx_in0"), sem("ctx_in1"), sem("ctx_in_lead")]
        var_ready = sem("var_ready")
        std_ready = sem("std_ready")
        bn_ready = sem("bn_ready")
        r_ready = sem("r_ready")
        mr_ready = sem("mr_ready")
        zc_ready = sem("zc_ready")
        z_ready = sem("z_ready")
        zT_ready = sem("zT_ready")
        hi_ready = sem("hi_ready")
        lo_ready = sem("lo_ready")
        k_ready = sem("k_ready")
        sq_ready = sem("sq_ready")
        n2_ready = sem("n2_ready")
        nrm_ready = sem("nrm_ready")
        floor_ready = sem("floor_ready")
        rinv_ready = sem("rinv_ready")
        kn_ready = sem("kn_ready")
        g_added = sem("g_added")
        fold_ready = sem("fold_ready")
        wkf_ready = sem("wkf_ready")
        wk_hi_ready = sem("wk_hi_ready")
        wk_lo_ready = sem("wk_lo_ready")
        wvf_ready = sem("wvf_ready")
        wv_ready = sem("wv_ready")
        x_stat = sem("x_stat")
        x_std_ready = sem("x_std_ready")
        xq_ready = sem("xq_ready")
        xqT_ps = sem("xqT_ps")
        xqT_ready = sem("xqT_ready")
        q_ready = sem("q_ready")
        q_sq_ready = sem("q_sq_ready")
        q_n2_ready = sem("q_n2_ready")
        q_nrm_ready = sem("q_nrm_ready")
        q_step = sem("q_step")
        qn_ready = sem("qn_ready")
        qnT_ps = sem("qnT_ps")
        qnT_ready = sem("qnT_ready")
        res_ready = sem("res_ready")
        pool_step = sem("pool_step")
        w1g_ready = sem("w1g_ready")
        fc1_ready = sem("fc1_ready")
        fc2_ready = sem("fc2_ready")
        decay_ready = sem("decay_ready")
        zero_ready = sem("zero_ready")
        eps_ready = sem("eps_ready")
        warm_done = sem("warm_done")
        bias_ps = sem("bias_ps")
        bias_col = sem("bias_col")
        biasT_ps = sem("biasT_ps")
        biasT_ready = sem("biasT_ready")
        gT_ready = sem("gT_ready")
        m_ready = sem("m_ready")
        mbd_ready = sem("mbd_ready")
        oT_ps = sem("oT_ps")
        oT_ready = sem("oT_ready")
        y1_ready = sem("y1_ready")
        x_ready = sem("x_ready")
        tbn_ready = sem("tbn_ready")
        tmv_ready = sem("tmv_ready")
        ve_ready = sem("ve_ready")
        tr_ready = sem("tr_ready")
        hat_ready = sem("hat_ready")
        hatT_ps = sem("hatT_ps")
        hatT_ready = sem("hatT_ready")
        h1_ps = sem("h1_ps")
        h1_ready = sem("h1_ready")
        y2_ready = sem("y2_ready")
        rest_ready = sem("rest_ready")
        u_ready = sem("u_ready")
        qkv_ps = sem("qkv_ps")
        qk_ready = sem("qk_ready")
        v_ready = sem("v_ready")
        s_ps = sem("s_ps")
        s_ready = sem("s_ready")
        ao_ps = sem("ao_ps")
        ao_ready = sem("ao_ready")
        aoT_ps = sem("aoT_ps")
        aoT_ready = sem("aoT_ready")
        y3_ready = sem("y3_ready")
        h2_ps = sem("h2_ps")
        h2_ready = sem("h2_ready")
        y4_ready = sem("y4_ready")
        final_ready = sem("final_ready")
        stored = sem("stored")

        ctx_v = ctx_rows.rearrange("(p t) d -> p t d", t=TILES)
        heads = lambda ap: ap.rearrange("p (h d) -> p h d", h=XH)

        def where(s_in_body):
            return (s_in_body // GROUP) % 2, s_in_body % GROUP

        block = ctx.enter_context(nc.Block())

        @block.sync
        def _(sp):
            sp.dma_start(ctx_s[:, 2, 0:1, :], ctx_v[:, 0:1, :]).then_inc(ctx_in[2], 16)
            sp.dma_start(col[:, :], cols).then_inc(in_small, 16)
            sp.dma_start(wk_s[:, :], wk).then_inc(in_wk, 16)
            for g in range(2):
                sp.dma_start(ctx_s[:, g, :, :], ctx_v[:, 1 + GROUP * g:1 + GROUP * (g + 1), :]).then_inc(ctx_in[g], 16)
            sp.dma_start(wv_s[:, :], wv).then_inc(in_wv, 16)
            sp.dma_start(fc2_q[:, :, :], fc2.rearrange("(c p) n -> p c n", c=MC)).then_inc(in_pool_w, 16)
            sp.dma_start(wo_s[:, :, :], wo.rearrange("(c p) n -> p c n", c=PAIRS)).then_inc(in_tail_w, 16)
            sp.dma_start(w2_s[:, :, :], w2.rearrange("(c p) n -> p c n", c=MC)).then_inc(in_tail_w, 16)
            for n, w in enumerate((wqT, wkT, wvT, woT)):
                sp.dma_start(attn_w[:, n, :], w).then_inc(in_tail_w, 16)
            with sp.Fori(0, ITERS - 1) as i:
                for g in range(2):
                    sp.wait_ge(z_ready, i * BODY + 1 + GROUP * (g + 1))
                    first = i * BODY + 1 + GROUP * (2 + g)
                    sp.dma_start(ctx_s[:, g, :, :], ctx_v[:, bass.ds(first, GROUP), :]).then_inc(ctx_in[g], 16)
            sp.wait_ge(final_ready, 1)
            sp.dma_start(out, y_out[:, :]).then_inc(stored, 16)
            sp.wait_ge(stored, 16)

        @block.gpsimd
        def _(pool):
            pool.dma_start(row[:, :], rows.partition_broadcast(P)).then_inc(in_row, 16)

            nc.gpsimd.memset(half_neg[:, :], -0.5).then_inc(pool_step, 1)
            nc.gpsimd.memset(m_bd[:, :, :], 0.0).then_inc(zero_ready, 1)
            nc.gpsimd.memset(ones_row[:, :], 1.0).then_inc(zero_ready, 1)
            pool.wait_ge(in_small, 32)
            pool.wait_ge(in_pool_w, 48)
            pool.wait_ge(in_row, 16)
            nc.gpsimd.tensor_scalar(w1_g[:, :], w1_s[:, :], col[:, 2:3], 0.0, ALU.mult, ALU.add).then_inc(w1g_ready, 1)
            nc.gpsimd.tensor_scalar(fc1_f[:, :], fc1_q[:, :], -128.0, 1.0, ALU.add, ALU.mult).then_inc(pool_step, 1)
            nc.gpsimd.tensor_scalar(fc2_f[:, :, :], fc2_q[:, :, :], -128.0, 1.0, ALU.add, ALU.mult).then_inc(pool_step, 1)
            pool.wait_ge(pool_step, 2)
            nc.gpsimd.tensor_tensor(fc1_d[:, :], fc1_f[:, :], row[:, R_S1:R_S1 + MLP], ALU.mult).then_inc(pool_step, 1)
            pool.wait_ge(pool_step, 3)
            nc.gpsimd.tensor_tensor(fc2_d[:, :, :], fc2_f[:, :, :],
                                    row[:, R_S2:R_S2 + MLP].rearrange("p (c n) -> p c n", c=MC),
                                    ALU.mult).then_inc(fc2_ready, 1)
            pool.wait_ge(pool_step, 4)
            nc.gpsimd.tensor_scalar(fc1_g[:, :], fc1_d[:, :], col[:, 4:5], 0.0, ALU.mult, ALU.add).then_inc(fc1_ready, 1)
            nc.gpsimd.tensor_tensor(decay[:, :], row[0:TOK, R_GAM:R_GAM + AH], cst[0:TOK, C_IDX:C_IDX + AH],
                                    ALU.pow).then_inc(decay_ready, 1)
            for n in range(3):
                w = 2 if n == 2 else 1
                pool.wait_ge(ve_ready, (1, 2, 4)[n])
                nc.gpsimd.tensor_tensor(t_r[:, n, 0:w], t_ve[:, n, 0:w], half_neg[:, 0:w], ALU.pow).then_inc(tr_ready, 1)

        @block.scalar
        def _(act):
            act.dma_start(xs[:, :], x).then_inc(in_x, 16)
            act.dma_start(cst[:, :], consts).then_inc(in_small, 16)
            act.dma_start(wq_s[:, :], wq).then_inc(in_wq, 16)
            act.dma_start(w1_s[:, :], w1).then_inc(in_pool_w, 16)
            act.dma_start(fc1_q[:, :], fc1).then_inc(in_pool_w, 16)
            act.dma_start(sel[:, :], chunk_select).then_inc(in_tail_w, 16)

            def group_std(slot, count, group):
                act.wait_ge(var_ready, group + 2)
                nc.scalar.activation(ln_std[:, slot, 0:count], mv[:, slot, 0:count, 1], ACT.Sqrt, bias=eps_c(0),
                                     scale=1.0).then_inc(std_ready, 1)

            def z_high(slot, count, group):
                act.wait_ge(zT_ready, group + 2)
                nc.scalar.activation(zT_hi[:, slot, 0:count * P], zT_ps[:, 0:count * P],
                                     ACT.Copy).then_inc(hi_ready, 1)

            def make_z(slot, places, group):
                act.wait_ge(zc_ready, group + 2)
                for j in places:
                    if not (type(group) is int and group < 2):
                        act.wait_ge(g_added, group * GROUP + (j + 2 - 2 * GROUP))
                    nc.scalar.activation(z[:, slot, j, :], ctx_s[:, slot, j, :], ACT.Identity,
                                         bias=ln_c[:, slot, j:j + 1], scale=ln_r[:, slot, j:j + 1]).then_inc(z_ready, 1)

            def square(s, buf):
                act.wait_ge(k_ready, s + 1)
                if not (type(s) is int and s < 2):
                    act.wait_ge(n2_ready, s - 1)
                nc.scalar.activation(k_sq[:, buf, :], k_ps[buf], ACT.Square).then_inc(sq_ready, 1)

            def norm(s, buf):
                act.wait_ge(n2_ready, s + 1)
                nc.scalar.activation(nrm[:, buf, :], n2[:, buf, :], ACT.Sqrt).then_inc(nrm_ready, 1)

            def eps_c(n, p=P):
                return eps_tile[0:p, n:n + 1]

            act.wait_ge(eps_ready, 2)
            act.wait_ge(x_stat, 2)
            nc.scalar.activation(x_std[:, 0:1], x_mv[:, 1:2], ACT.Sqrt, bias=eps_c(0, TOK),
                                 scale=1.0).then_inc(x_std_ready, 1)
            nc.scalar.activation(x_std[:, 1:2], x_mv[:, 1:2], ACT.Sqrt, bias=eps_c(1, TOK),
                                 scale=1.0 + EPS).then_inc(x_std_ready, 1)
            group_std(2, 1, -1)
            make_z(2, range(1), -1)
            group_std(0, GROUP, 0)
            act.wait_ge(wkf_ready, 1)
            nc.scalar.activation(wk_hi[:, :], k_ps[0], ACT.Copy).then_inc(wk_hi_ready, 1)
            z_high(2, 1, -1)
            make_z(0, range(GROUP), 0)
            square(0, 0)
            z_high(0, GROUP, 0)
            act.wait_ge(q_ready, 1)
            nc.scalar.activation(q_sq[:, :], ps[0:TOK, 0:2, :], ACT.Square).then_inc(q_sq_ready, 1)
            norm(0, 0)
            act.wait_ge(wvf_ready, 1)
            nc.scalar.activation(wv_f[:, :], k_ps[1], ACT.Copy).then_inc(wv_ready, 1)
            act.wait_ge(q_n2_ready, 1)
            nc.scalar.activation(q_n2[:, 1, :], q_n2[:, 0, :], ACT.Sqrt).then_inc(q_nrm_ready, 1)

            def body(i, last=False):
                for j in range(BODY):
                    s = i * BODY + (1 + j)
                    slot, place = where(j + GROUP)
                    group = i * 2 + (j // GROUP + 1)
                    prepare = not (last and j >= GROUP)
                    if place == 1 and prepare:
                        group_std(slot, GROUP, group)
                    if place == 3 and prepare:
                        z_high(slot, GROUP, group)
                    square(s, (1 + j) % 2)
                    if place == 2 and prepare:
                        make_z(slot, range(2, GROUP), group)
                    norm(s, (1 + j) % KN)
                    if place == 1 and prepare:
                        make_z(slot, range(2), group)

            body(0)
            with act.Fori(1, ITERS - 1) as i:
                body(i)
            body(ITERS - 1, last=True)
            act.wait_ge(pool_step, 1)
            nc.scalar.activation(warm[:, 0:1], half_neg[:, 0:1], ACT.Gelu).then_inc(warm_done, 1)
            act.wait_ge(g_added, TILES)
            nc.scalar.activation(gT[:, 0:HALF], ps[:, 0, :], ACT.Copy).then_inc(gT_ready, 1)
            act.wait_ge(m_ready, 1)
            act.wait_ge(zero_ready, 1)
            nc.scalar.activation(m_bd[0:XD, :, 0:XD],
                                 ps[0:XD, 2:4, :].rearrange("p b (c n) -> p (b c) n", n=P)[:, :, 0:XD],
                                 ACT.Copy).then_inc(mbd_ready, 1)
            act.wait_ge(oT_ps, 1)
            nc.scalar.activation(oT[:, 0:PAIRS // 2, :], ps[:, 4, 0:256], ACT.Copy).then_inc(oT_ready, 1)
            act.wait_ge(h1_ps, 1)
            nc.scalar.activation(h1[:, :], ps[:, 7, 0:MC * TOK], ACT.Gelu).then_inc(h1_ready, 1)
            act.wait_ge(warm_done, 1)
            nc.scalar.activation(warm[:, 1:2], half_neg[:, 0:1], ACT.Silu).then_inc(warm_done, 1)
            act.wait_ge(qkv_ps, 3)
            nc.scalar.activation(v_s[:, :], ps[:, 1, 256:384], ACT.Copy).then_inc(v_ready, 1)
            act.wait_ge(h2_ps, 1)
            nc.scalar.activation(h2[:, :], ps[:, 7, 0:MC * TOK], ACT.Silu).then_inc(h2_ready, 1)

        @block.vector
        def _(dve):
            def stats(slot, count):
                for j in range(count):
                    last = nc.vector.bn_stats(bn[:, slot, j, :], ctx_s[:, slot, j, :])
                last.then_inc(bn_ready, 1)

            def aggregate(slot, count):
                for j in range(count):
                    last = nc.vector.bn_aggr(mv[:, slot, j, :], bn[:, slot, j, :])
                last.then_inc(var_ready, 1)

            def z_scalars(slot, count, group):
                dve.wait_ge(std_ready, group + 2)
                nc.vector.reciprocal(ln_r[:, slot, 0:count], ln_std[:, slot, 0:count]).then_inc(r_ready, 1)
                dve.wait_ge(r_ready, group + 2)
                nc.vector.tensor_tensor(ln_mr[:, slot, 0:count], mv[:, slot, 0:count, 0], ln_r[:, slot, 0:count],
                                        ALU.mult).then_inc(mr_ready, 1)
                dve.wait_ge(mr_ready, group + 2)
                nc.vector.tensor_scalar(ln_c[:, slot, 0:count], ln_mr[:, slot, 0:count], -1.0, 1.0,
                                        ALU.mult, ALU.add).then_inc(zc_ready, 1)

            def z_low(slot, count, group):
                dve.wait_ge(hi_ready, group + 2)
                nc.vector.tensor_tensor(zT_lo[:, slot, 0:count * P], zT_ps[:, 0:count * P],
                                        zT_hi[:, slot, 0:count * P].bitcast(F32), ALU.subtract).then_inc(lo_ready, 1)

            def head_sums(s, sq, buf):
                dve.wait_ge(sq_ready, s + 1)
                nc.vector.tensor_reduce(n2[:, buf, :], heads(k_sq[:, sq, :]), AX_X, ALU.add).then_inc(n2_ready, 1)

            def normalise(s, kbuf, buf, stats_of=None):
                if stats_of is not None:
                    dve.wait_ge(bn_ready, stats_of + 2)
                dve.wait_ge(nrm_ready, s + 1)
                nc.vector.tensor_scalar(nrm_floor[:, buf, :], nrm[:, buf, :], TINY, None, ALU.max).then_inc(floor_ready, 1)
                dve.wait_ge(floor_ready, s + 1)
                nc.vector.reciprocal(rinv[:, buf, :], nrm_floor[:, buf, :]).then_inc(rinv_ready, 1)
                dve.wait_ge(rinv_ready, s + 1)
                if not (type(s) is int and s < KN):
                    dve.wait_ge(g_added, s - KN + 1)
                nc.vector.tensor_tensor(
                    heads(kn[:, buf, :]),
                    k_ps[kbuf].rearrange("p b (h d) -> p (b h) d", d=XD),
                    rinv[:, buf, :].unsqueeze(2).broadcast_to([P, XH, XD]),
                    ALU.mult).then_inc(kn_ready, 1)

            nc.vector.memset(eps_tile[:, 0:1], EPS).then_inc(eps_ready, 1)
            nc.vector.memset(eps_tile[:, 1:2], EPS * EPS).then_inc(eps_ready, 1)
            dve.wait_ge(in_x, 16)
            nc.vector.bn_stats(x_bn[:, :], xs[:, :]).then_inc(x_stat, 1)
            dve.wait_ge(x_stat, 1)
            nc.vector.bn_aggr(x_mv[:, :], x_bn[:, :]).then_inc(x_stat, 1)
            dve.wait_ge(ctx_in[2], 16)
            stats(2, 1)
            dve.wait_ge(bn_ready, 1)
            aggregate(2, 1)
            dve.wait_ge(in_small, 32)
            nc.vector.tensor_tensor(fold_d[:, 0:1], col[:, 1:2], col[:, 0:1], ALU.subtract).then_inc(fold_ready, 1)
            dve.wait_ge(fold_ready, 1)
            nc.vector.tensor_scalar(fold_d[:, 1:2], fold_d[:, 0:1], 1.0 / D, None, ALU.mult).then_inc(fold_ready, 1)
            dve.wait_ge(fold_ready, 2)
            nc.vector.tensor_scalar(fold[:, :], ident, col[:, 0:1], fold_d[:, 1:2], ALU.mult, ALU.add).then_inc(fold_ready, 1)
            z_scalars(2, 1, -1)
            dve.wait_ge(x_std_ready, 2)
            nc.vector.reciprocal(x_r[:, :], x_std[:, :]).then_inc(x_stat, 1)
            dve.wait_ge(x_stat, 3)
            nc.vector.tensor_scalar(xq[:, :], xs[:, :], x_mv[:, 0:1], x_r[:, 1:2], ALU.subtract, ALU.mult).then_inc(xq_ready, 1)
            nc.vector.tensor_scalar(xl[:, :], xs[:, :], x_mv[:, 0:1], x_r[:, 0:1], ALU.subtract, ALU.mult).then_inc(x_stat, 1)
            dve.wait_ge(ctx_in[0], 16)
            stats(0, GROUP)
            dve.wait_ge(bn_ready, 2)
            aggregate(0, GROUP)
            z_scalars(0, GROUP, 0)
            dve.wait_ge(xqT_ps, 1)
            nc.vector.tensor_scalar(xqT[:, :], misc[:, 0:TOK], col[:, 0:1], col[:, 1:2], ALU.mult, ALU.add).then_inc(xqT_ready, 1)
            dve.wait_ge(wk_hi_ready, 1)
            nc.vector.tensor_tensor(wk_lo[:, :], k_ps[0], wk_hi[:, :].bitcast(F32), ALU.subtract).then_inc(wk_lo_ready, 1)
            z_low(2, 1, -1)
            head_sums(0, 0, 0)
            z_low(0, GROUP, 0)
            normalise(0, 0, 0)
            dve.wait_ge(q_sq_ready, 1)
            nc.vector.tensor_reduce(q_n2[:, 0, :], heads(q_sq[:, :]), AX_X, ALU.add).then_inc(q_n2_ready, 1)
            dve.wait_ge(q_nrm_ready, 1)
            nc.vector.tensor_scalar(q_n2[:, 2, :], q_n2[:, 1, :], TINY, None, ALU.max).then_inc(q_step, 1)
            dve.wait_ge(q_step, 1)
            nc.vector.reciprocal(q_n2[:, 3, :], q_n2[:, 2, :]).then_inc(q_step, 1)
            dve.wait_ge(q_step, 2)
            nc.vector.tensor_tensor(heads(qn[:, :]), ps[0:TOK, 0:2, :].rearrange("p b (h d) -> p (b h) d", d=XD),
                                    q_n2[:, 3, :].unsqueeze(2).broadcast_to([TOK, XH, XD]), ALU.mult).then_inc(qn_ready, 1)
            dve.wait_ge(qnT_ps, 1)
            nc.vector.tensor_copy(qnT[:, :, :], misc.rearrange("p (c t) -> p c t", c=PAIRS)).then_inc(qnT_ready, 1)
            dve.wait_ge(in_row, 16)
            dve.wait_ge(x_stat, 4)
            nc.vector.tensor_tensor(xl_bo[:, :], xl[:, :], row[0:TOK, R_BO:R_BO + D], ALU.add).then_inc(res_ready, 1)
            nc.vector.tensor_tensor(x_b2[:, :], xs[:, :], row[0:TOK, R_B2:R_B2 + D], ALU.add).then_inc(res_ready, 1)
            nc.vector.tensor_scalar(fb_half[:, :], row[0:TOK, R_FB2:R_FB2 + D], 0.5, None, ALU.mult).then_inc(res_ready, 1)

            def body(i, last=False):
                for j in range(BODY):
                    s = i * BODY + (1 + j)
                    slot, place = where(j + GROUP)
                    group = i * 2 + (j // GROUP + 1)
                    prepare = not (last and j >= GROUP)
                    if place == 3 and prepare:
                        z_low(slot, GROUP, group)
                    head_sums(s, (1 + j) % 2, (1 + j) % KN)
                    if place == 0 and prepare:
                        dve.wait_ge(ctx_in[slot], (i + (j // GROUP + 1) // 2 + 1) * 16)
                        stats(slot, GROUP)
                    if place == 1 and prepare:
                        z_scalars(slot, GROUP, group)
                    starts = place == 0 and prepare
                    normalise(s, (1 + j) % 2, (1 + j) % KN, group if starts else None)
                    if starts:
                        aggregate(slot, GROUP)

            body(0)
            dve.wait_ge(bias_ps, 1)
            nc.vector.tensor_tensor(bias_c[:, :], misc[:, 0:2 * MC], col[:, 8:8 + 2 * MC], ALU.add).then_inc(bias_col, 1)
            dve.wait_ge(biasT_ps, 1)
            nc.vector.tensor_copy(biasT[:, :], misc[0:2 * MC, 0:P]).then_inc(biasT_ready, 1)
            with dve.Fori(1, ITERS - 1) as i:
                body(i)
            body(ITERS - 1, last=True)

            def layernorm(n, src):
                dve.wait_ge(x_ready, n + 1)
                nc.vector.bn_stats(t_bn[:, n, :], src).then_inc(tbn_ready, 1)
                dve.wait_ge(tbn_ready, n + 1)
                nc.vector.bn_aggr(t_mv[:, n, :], t_bn[:, n, :]).then_inc(tmv_ready, 1)
                dve.wait_ge(tmv_ready, n + 1)
                nc.vector.tensor_scalar(t_ve[:, n, 0:1], t_mv[:, n, 1:2], EPS, None, ALU.add).then_inc(ve_ready, 1)
                if n == 2:
                    nc.vector.tensor_scalar(t_ve[:, n, 1:2], t_mv[:, n, 1:2], 1.0 + EPS, EPS * EPS,
                                            ALU.mult, ALU.add).then_inc(ve_ready, 1)
                dve.wait_ge(tr_ready, n + 1)
                which = 1 if n == 2 else 0
                nc.vector.tensor_scalar(t_hat[:, n, :], src, t_mv[:, n, 0:1], t_r[:, n, which:which + 1],
                                        ALU.subtract, ALU.mult).then_inc(hat_ready, 1)

            dve.wait_ge(g_added, TILES)
            nc.vector.tensor_copy(gT[:, HALF:INNER], ps[:, 1, :]).then_inc(gT_ready, 1)
            dve.wait_ge(m_ready, 1)
            dve.wait_ge(zero_ready, 1)
            nc.vector.tensor_copy(m_bd[XD:P, :, XD:P],
                                  ps[XD:P, 2:4, :].rearrange("p b (c n) -> p (b c) n", n=P)[:, :, XD:P]
                                  ).then_inc(mbd_ready, 1)
            dve.wait_ge(oT_ps, 1)
            nc.vector.tensor_copy(oT[:, PAIRS // 2:PAIRS, :], ps[:, 5, 0:256].rearrange("p (c t) -> p c t", t=TOK)
                                  ).then_inc(oT_ready, 1)
            dve.wait_ge(y1_ready, 1)
            dve.wait_ge(res_ready, 3)
            nc.vector.tensor_tensor(x1[:, :], ps[0:TOK, 6, 0:D], xl_bo[:, :], ALU.add).then_inc(x_ready, 1)
            layernorm(0, x1[:, :])
            nc.vector.tensor_tensor(x1_r[:, :], x1[:, :], x_b2[:, :], ALU.add).then_inc(rest_ready, 1)
            dve.wait_ge(hatT_ps, 1)
            nc.vector.tensor_copy(hatT[:, 0, 0:TOK], ps[:, 6, 0:TOK]).then_inc(hatT_ready, 1)
            dve.wait_ge(y2_ready, 1)
            dve.wait_ge(rest_ready, 1)
            nc.vector.tensor_tensor(x2[:, :], ps[0:TOK, 0, 0:D], x1_r[:, :], ALU.add).then_inc(x_ready, 1)
            layernorm(1, x2[:, :])
            nc.vector.tensor_tensor(x2_r[:, :], x2[:, :], row[0:TOK, R_ABO:R_ABO + D], ALU.add).then_inc(rest_ready, 1)
            dve.wait_ge(hatT_ps, 2)
            nc.vector.tensor_copy(hatT[:, 1, :].rearrange("p (a t) -> p a t", a=2),
                                  ps[:, 6, 0:TOK].unsqueeze(1).broadcast_to([P, 2, TOK])).then_inc(hatT_ready, 1)
            dve.wait_ge(qkv_ps, 1)
            nc.vector.scalar_tensor_tensor(
                q_heads[:, :, :], ps[:, 7, 0:TOK].unsqueeze(1).broadcast_to([P, ROWG, TOK]), col[:, 6:7],
                cst[:, C_HEAD:C_HEAD + ROWG].unsqueeze(2).broadcast_to([P, ROWG, TOK]),
                ALU.add, ALU.mult).then_inc(qk_ready, 1)
            dve.wait_ge(qkv_ps, 2)
            nc.vector.scalar_tensor_tensor(
                k_groups[:, :, :], ps[:, 5, 0:TOK].unsqueeze(1).broadcast_to([P, ROWG, TOK]), col[:, 7:8],
                cst[:, C_GRP:C_GRP + ROWG].unsqueeze(2).broadcast_to([P, ROWG, TOK]),
                ALU.add, ALU.mult).then_inc(qk_ready, 1)
            dve.wait_ge(s_ps, 1)
            nc.vector.tensor_tensor(scores[:, :, :], ps[:, 2, :].rearrange("p (c t) -> p c t", t=TOK),
                                    cst[:, C_CAUSAL:C_CAUSAL + TOK].unsqueeze(1).broadcast_to([P, 8, TOK]),
                                    ALU.mult).then_inc(s_ready, 1)
            dve.wait_ge(ao_ps, 1)
            dve.wait_ge(decay_ready, 1)
            for n in range(2):
                nc.vector.tensor_tensor(
                    a_out[:, TOK * n:TOK * (n + 1)].rearrange("p (h d) -> p h d", d=AD),
                    ps[0:TOK, 3 + n, 0:TOK].rearrange("p (h d) -> p h d", d=AD),
                    decay[:, 8 * n:8 * n + 8].unsqueeze(2).broadcast_to([TOK, 8, AD]),
                    ALU.mult).then_inc(ao_ready, 1)
            dve.wait_ge(aoT_ps, 1)
            nc.vector.tensor_copy(a_outT[:, :], ps[:, 6, 0:TOK]).then_inc(aoT_ready, 1)
            dve.wait_ge(y3_ready, 1)
            dve.wait_ge(rest_ready, 2)
            nc.vector.tensor_tensor(x3[:, :], ps[0:TOK, 0, 0:D], x2_r[:, :], ALU.add).then_inc(x_ready, 1)
            layernorm(2, x3[:, :])
            nc.vector.tensor_scalar(u[:, :], x3[:, :], t_mv[:, 2, 0:1], t_r[:, 2, 0:1],
                                    ALU.subtract, ALU.mult).then_inc(u_ready, 1)
            dve.wait_ge(hatT_ps, 3)
            nc.vector.tensor_copy(hatT[:, 2, 0:TOK], ps[:, 6, 0:TOK]).then_inc(hatT_ready, 1)
            dve.wait_ge(u_ready, 1)
            nc.vector.tensor_tensor(x3_u[:, :], x3[:, :], u[:, :], ALU.add).then_inc(u_ready, 1)
            dve.wait_ge(u_ready, 2)
            nc.vector.tensor_tensor(x3_r[:, :], x3_u[:, :], fb_half[:, :], ALU.add).then_inc(rest_ready, 1)
            dve.wait_ge(y4_ready, 1)
            dve.wait_ge(rest_ready, 3)
            nc.vector.scalar_tensor_tensor(y_out[:, :], ps[0:TOK, 1, 0:D], 0.5, x3_r[:, :],
                                           ALU.mult, ALU.add).then_inc(final_ready, 1)

        @block.tensor
        def _(pe):
            mm = nc.tensor.matmul

            def transposes(slot, count, group):
                pe.wait_ge(z_ready, GROUP * group + (GROUP + 1))
                for j in range(count):
                    last = nc.tensor.transpose(zT_ps[:, j * P:(j + 1) * P], z[:, slot, j, :], ident)
                last.then_inc(zT_ready, 1)

            def keys(s, buf, slot, place, group):
                if place == 0:
                    pe.wait_ge(hi_ready, group + 2)
                    pe.wait_ge(lo_ready, group + 2)
                if not (type(s) is int and s < 2):
                    pe.wait_ge(kn_ready, s - 1)
                hi = zT_hi[:, slot, place * P:(place + 1) * P]
                lo = zT_lo[:, slot, place * P:(place + 1) * P]
                for half in range(2):
                    c = slice(half * HALF, (half + 1) * HALF)
                    o = k_ps[buf][:, half, :]
                    mm(o, hi, wk_lo[:, c], start=True, stop=False)
                    mm(o, lo, wk_hi[:, c], start=False, stop=False)
                    last = mm(o, hi, wk_hi[:, c], start=False, stop=True)
                last.then_inc(k_ready, 1)

            def add_g(s, buf, slot, place, first=False, final=False):
                pe.wait_ge(kn_ready, s + 1)
                for half in range(2):
                    last = mm(g_ps[:, half, :], z[:, slot, place, :], kn[:, buf, half * HALF:(half + 1) * HALF],
                              start=first, stop=final)
                last.then_inc(g_added, 1)

            pe.wait_ge(fold_ready, 3)
            pe.wait_ge(in_wk, 16)
            for half in range(2):
                last = mm(k_ps[0][:, half, :], fold[:, :], wk_s[:, half * HALF:(half + 1) * HALF], start=True, stop=True)
            last.then_inc(wkf_ready, 1)
            transposes(2, 1, -1)
            pe.wait_ge(xq_ready, 1)
            nc.tensor.transpose(misc[:, 0:TOK], xq[:, :], ident[0:TOK, 0:TOK]).then_inc(xqT_ps, 1)
            pe.wait_ge(wk_lo_ready, 1)
            keys(0, 0, 2, 0, -1)
            transposes(0, GROUP, 0)
            pe.wait_ge(xqT_ready, 1)
            pe.wait_ge(in_wq, 16)
            for half in range(2):
                last = mm(ps[0:TOK, half, :], xqT[:, :], wq_s[:, half * HALF:(half + 1) * HALF], start=True, stop=True)
            last.then_inc(q_ready, 1)
            pe.wait_ge(in_wv, 16)
            for half in range(2):
                last = mm(k_ps[1][:, half, :], fold[:, :], wv_s[:, half * HALF:(half + 1) * HALF], start=True, stop=True)
            last.then_inc(wvf_ready, 1)
            pe.wait_ge(qn_ready, 1)
            for c in range(PAIRS):
                last = nc.tensor.transpose(misc[:, c * TOK:(c + 1) * TOK], qn[:, c * P:(c + 1) * P], ident[0:TOK, 0:TOK])
            last.then_inc(qnT_ps, 1)
            pe.wait_ge(wv_ready, 1)

            def body(i, first=False, last=False):
                for j in range(BODY):
                    s = i * BODY + (1 + j)
                    slot, place = where(j)
                    group = i * 2 + j // GROUP
                    if place == 3 and not (last and j >= GROUP):
                        transposes(where(j + GROUP)[0], GROUP, group + 1)
                    keys(s, (1 + j) % 2, slot, place, group)
                    if first and j < 2:
                        if j == 1:
                            add_g(0, 0, 2, 0, first=True)
                        continue
                    add_g(s - 2, (j - 1) % KN, *where((j - 2) % BODY))

            body(0, first=True)
            pe.wait_ge(in_pool_w, 48)
            pe.wait_ge(fc1_ready, 1)
            pe.wait_ge(qnT_ready, 1)
            for c in range(MC):
                mm(misc[:, c:c + 1], w1_s[:, c * P:(c + 1) * P], col[:, 3:4], start=True, stop=True)
            for c in range(MC):
                last = mm(misc[:, MC + c:MC + c + 1], fc1_d[:, c * P:(c + 1) * P], col[:, 5:6], start=True, stop=True)
            last.then_inc(bias_ps, 1)
            pe.wait_ge(bias_col, 1)
            nc.tensor.transpose(misc[0:2 * MC, 0:P], bias_c[:, :], ident).then_inc(biasT_ps, 1)
            with pe.Fori(1, ITERS - 1) as i:
                body(i)
            body(ITERS - 1, last=True)
            add_g(TILES - 2, (TILES - 2) % KN, *where(BODY - 2))
            add_g(TILES - 1, (TILES - 1) % KN, *where(BODY - 1), final=True)

            pe.wait_ge(gT_ready, 2)
            for c in range(PAIRS):
                last = mm(ps[:, 2 + c // 4, (c % 4) * P:(c % 4 + 1) * P], gT[:, c * P:(c + 1) * P],
                          wv_f[:, c * P:(c + 1) * P], start=True, stop=True)
            last.then_inc(m_ready, 1)
            pe.wait_ge(mbd_ready, 2)
            for c in range(PAIRS):
                last = mm(ps[:, 4 + c // 4, (c % 4) * TOK:(c % 4 + 1) * TOK], m_bd[:, c, :], qnT[:, c, :], start=True, stop=True)
            last.then_inc(oT_ps, 1)
            pe.wait_ge(oT_ready, 2)
            pe.wait_ge(in_tail_w, 16 * 7)
            for c in range(PAIRS):
                last = mm(ps[0:TOK, 6, 0:D], oT[:, c, :], wo_s[:, c, :], start=(c == 0), stop=(c == PAIRS - 1))
            last.then_inc(y1_ready, 1)

            def hat_transpose(n):
                pe.wait_ge(hat_ready, n + 1)
                nc.tensor.transpose(ps[:, 6, 0:TOK], t_hat[:, n, :], ident[0:TOK, 0:TOK]).then_inc(hatT_ps, 1)

            def hidden_bias(n):
                pe.wait_ge(biasT_ready, 1)
                mm(ps[:, 7, 0:MC * TOK], biasT[:, :], sel[:, n * MC * TOK:(n + 1) * MC * TOK], start=True, stop=False,
                   skip_group_check=True)

            hidden_bias(0)
            hat_transpose(0)
            pe.wait_ge(hatT_ready, 1)
            for c in range(MC):
                last = mm(ps[:, 7, c * TOK:(c + 1) * TOK], w1_g[:, c * P:(c + 1) * P], hatT[:, 0, 0:TOK],
                          start=False, stop=(c == MC - 1), skip_group_check=True)
            last.then_inc(h1_ps, 1)
            pe.wait_ge(h1_ready, 1)
            for c in range(MC):
                last = mm(ps[0:TOK, 0, 0:D], h1[:, c * TOK:(c + 1) * TOK], w2_s[:, c, :], start=(c == 0), stop=(c == MC - 1))
            last.then_inc(y2_ready, 1)
            hat_transpose(1)
            pe.wait_ge(hatT_ready, 2)
            mm(ps[:, 7, 0:TOK], attn_w[:, 0, :], hatT[:, 1, 0:TOK], start=True, stop=True).then_inc(qkv_ps, 1)
            mm(ps[:, 5, 0:TOK], attn_w[:, 1, :], hatT[:, 1, 0:TOK], start=True, stop=True).then_inc(qkv_ps, 1)
            pe.wait_ge(in_row, 16)
            pe.wait_ge(zero_ready, 2)
            mm(ps[:, 1, 256:384], hatT[:, 1, :], attn_w[:, 2, :], start=True, stop=False)
            mm(ps[:, 1, 256:384], ones_row[0:1, :], row[0:1, R_BV:R_BV + D], start=False, stop=True).then_inc(qkv_ps, 1)
            pe.wait_ge(qk_ready, 2)
            for g in range(ROWG):
                at = 64 * (g // 2)
                last = mm(ps[at:at + TOK, 2, 256 * (g % 2):256 * (g % 2) + 256], k_groups[:, g, :],
                          q_heads[:, :, :], start=True, stop=True)
            last.then_inc(s_ps, 1)
            pe.wait_ge(s_ready, 1)
            pe.wait_ge(v_ready, 1)
            for h in range(AH):
                at = 64 * (h // 8)
                last = mm(ps[0:TOK, 3 + h // 8, AD * (h % 8):AD * (h % 8) + AD], scores[at:at + TOK, h % 8, :],
                          v_s[at:at + TOK, AD * h:AD * h + AD], start=True, stop=True)
            last.then_inc(ao_ps, 1)
            pe.wait_ge(ao_ready, 2)
            nc.tensor.transpose(ps[:, 6, 0:TOK], a_out[:, :], ident[0:TOK, 0:TOK]).then_inc(aoT_ps, 1)
            pe.wait_ge(aoT_ready, 1)
            mm(ps[0:TOK, 0, 0:D], a_outT[:, :], attn_w[:, 3, :], start=True, stop=True).then_inc(y3_ready, 1)
            hidden_bias(1)
            hat_transpose(2)
            pe.wait_ge(hatT_ready, 3)
            for c in range(MC):
                last = mm(ps[:, 7, c * TOK:(c + 1) * TOK], fc1_g[:, c * P:(c + 1) * P], hatT[:, 2, 0:TOK],
                          start=False, stop=(c == MC - 1), skip_group_check=True)
            last.then_inc(h2_ps, 1)
            pe.wait_ge(h2_ready, 1)
            pe.wait_ge(fc2_ready, 1)
            for c in range(MC):
                last = mm(ps[0:TOK, 1, 0:D], h2[:, c * TOK:(c + 1) * TOK], fc2_d[:, c, :], start=(c == 0), stop=(c == MC - 1))
            last.then_inc(y4_ready, 1)


def kernel(x, ctx_1024, L0_xattn_wq, L0_xattn_wk, L0_xattn_wv, L0_xattn_wo, L0_xattn_bo, L0_xattn_w1, L0_xattn_b1,
           L0_xattn_w2, L0_xattn_b2, L0_xattn_ln1_g, L0_xattn_ln1_b, L0_xattn_ln2_g, L0_xattn_ln2_b, L0_attn_Wq,
           L0_attn_bq, L0_attn_Wk, L0_attn_bk, L0_attn_Wv, L0_attn_bv, L0_attn_Wo, L0_attn_bo, L0_attn_gamma,
           L0_ffn_ln_gamma, L0_ffn_ln_beta, L0_ffn_fc1_q, L0_ffn_fc1_scales, L0_ffn_fc1_bias, L0_ffn_fc2_q,
           L0_ffn_fc2_scales, L0_ffn_fc2_bias):
    import numpy as np
    import concourse.bacc as bacc
    from concourse import mybir as mb
    from concourse.bass_utils import run_bass_kernel_spmd

    lay = np.ascontiguousarray
    chunks = lambda v: np.asarray(v).reshape(MC, P).T
    column = lambda v: np.asarray(v).reshape(P, 1)
    cols = np.concatenate([column(v) for v in (L0_xattn_ln1_g, L0_xattn_ln1_b, L0_xattn_ln2_g, L0_xattn_ln2_b,
                                               L0_ffn_ln_gamma, L0_ffn_ln_beta, L0_attn_bq, L0_attn_bk)]
                          + [chunks(L0_xattn_b1), chunks(L0_ffn_fc1_bias)], axis=1)
    rows = np.concatenate([np.asarray(v).reshape(-1) for v in (
        L0_xattn_bo, L0_xattn_b2, L0_attn_bo, L0_ffn_fc2_bias, L0_attn_bv, L0_attn_gamma, L0_ffn_fc1_scales,
        L0_ffn_fc2_scales)])
    p = np.arange(P)
    consts = np.zeros((P, CCW), np.float32)
    consts[:, C_ID:C_ID + P] = np.eye(P)
    consts[:, C_CAUSAL:C_CAUSAL + TOK] = (p[:, None] % TOK) <= np.arange(TOK)[None, :]
    consts[:, C_HEAD:C_HEAD + ROWG] = (p[:, None] % (ROWG * AD)) // AD == np.arange(ROWG)[None, :]
    consts[:, C_GRP:C_GRP + ROWG] = p[:, None] // (ROWG * AD) == np.arange(ROWG)[None, :]
    consts[:, C_IDX:C_IDX + AH] = p[:, None]
    chunk_select = np.repeat(np.eye(2 * MC, dtype=np.float32), TOK, axis=1)

    arrays = {
        "x": lay(x[0]), "ctx": lay(ctx_1024[0]), "wq": lay(L0_xattn_wq), "wk": lay(L0_xattn_wk), "wv": lay(L0_xattn_wv),
        "wo": lay(L0_xattn_wo), "w1": lay(L0_xattn_w1), "w2": lay(L0_xattn_w2), "wqT": lay(np.asarray(L0_attn_Wq).T),
        "wkT": lay(np.asarray(L0_attn_Wk).T), "wvT": lay(np.asarray(L0_attn_Wv).T), "woT": lay(np.asarray(L0_attn_Wo).T),
        "fc1": lay(L0_ffn_fc1_q), "fc2": lay(L0_ffn_fc2_q), "cols": lay(cols), "rows": lay(rows), "consts": consts,
        "chunk_select": chunk_select,
    }
    nc = bacc.Bacc("TRN2", target_bir_lowering=False, num_devices=1)
    feeds, args = {}, []
    for name, a in arrays.items():
        feeds[f"in_{name}"] = a
        args.append(nc.dram_tensor(f"in_{name}", a.shape, mb.dt.from_np(a.dtype), kind="ExternalInput").ap())
    result = nc.dram_tensor("result", (1, TOK, D), mb.dt.float32, kind="ExternalOutput").ap()
    build_kernel(nc, *args, result[0])
    r = run_bass_kernel_spmd(nc, [feeds], core_ids=[0])
    return r.results[0]["result"]
```

```python
from contextlib import ExitStack

import concourse.bass as bass
from concourse import mybir

F32 = mybir.dt.float32
F32R = mybir.dt.float32r
I32 = mybir.dt.int32
ALU = mybir.AluOpType
ACT = mybir.ActivationFunctionType
AX_X = mybir.AxisListType.X

P = 128
D = 128
TOK = 64
CTX = 6272
TILES = CTX // P
GROUP = 4
BODY = 8
ITERS = (TILES - 1) // BODY
XH, XD = 16, 64
INNER = XH * XD
PAIRS = INNER // P
HALF = INNER // 2
MLP = 512
MC = MLP // P
AH, AD = 16, 8
ROWG = 4
EPS = 1e-5
TINY = 1e-12
KN = 4
WARM = 7

COLS = ["ln1_g", "ln1_b", "ln2_g", "ln2_b", "fln_g", "fln_b", "bq", "bk", "b1", "fc1_b", "gamma"]
CW = 9 + 2 * MC
C_B1 = 8
C_GAM = 8 + 2 * MC
R_BO, R_B2, R_ABO, R_FB2, R_BV, R_S1, R_S2 = 0, 128, 256, 384, 512, 640, 1152
RW = 1664
C_ID, C_CAUSAL, C_HEAD, C_GRP, C_H8, C_IDX = 0, 128, 192, 196, 200, 208
CCW = 272


def build_kernel(nc, x, ctx_rows, wq, wk, wv, wo, w1, w2, wqT, wkT, wvT, woT, fc1, fc2, cols_consts, rows,
                 chunk_select, out):
    ctx = ExitStack()
    with ctx:
        def sb(name, shape, dt=F32):
            return ctx.enter_context(nc.sbuf_tensor(name, shape, dt))

        def sem(name):
            return ctx.enter_context(nc.semaphore(name))

        cst_col = sb("cst_col", [P, CCW + CW])
        cst = cst_col[:, 0:CCW]
        col = cst_col[:, CCW:CCW + CW]
        row = sb("row", [P, RW])
        sel = sb("sel", [2 * MC, 2 * MC * TOK])
        xs = sb("xs", [TOK, D])
        wq_s = sb("wq_s", [P, INNER])
        wk_s = sb("wk_s", [P, INNER])
        wv_s = sb("wv_s", [P, INNER])
        wo_s = sb("wo_s", [P, PAIRS, D])
        w1_s = sb("w1_s", [P, MLP])
        w2_s = sb("w2_s", [P, MC, D])
        attn_w = sb("attn_w", [P, 4, D])
        fc1_q = sb("fc1_q", [P, MLP], I32)
        fc2_q = sb("fc2_q", [P, MC, D], I32)
        ident = cst[:, C_ID:C_ID + P]
        ctx_s = sb("ctx_s", [P, 3, GROUP, D])
        z = sb("z", [P, 3, GROUP, D])
        zT_hi = sb("zT_hi", [P, 3, GROUP * P], F32R)
        zT_lo = sb("zT_lo", [P, 3, GROUP * P], F32R)
        bn = sb("bn", [P, 3, GROUP, 6])
        mv = sb("mv", [P, 3, GROUP, 2])
        ln_std = sb("ln_std", [P, 3, GROUP])
        ln_r = sb("ln_r", [P, 3, GROUP])
        ln_mr = sb("ln_mr", [P, 3, GROUP])
        ln_c = sb("ln_c", [P, 3, GROUP])
        k_sq = sb("k_sq", [P, 2, INNER])
        n2 = sb("n2", [P, KN, XH])
        nrm = sb("nrm", [P, KN, XH])
        rinv = sb("rinv", [P, KN, XH])
        kn = sb("kn", [P, KN, INNER])
        fold_d = sb("fold_d", [P, 2])
        fold = sb("fold", [P, P])
        wk_hi = sb("wk_hi", [P, INNER], F32R)
        wk_lo = sb("wk_lo", [P, INNER], F32R)
        wv_f = sb("wv_f", [P, INNER])
        x_bn = sb("x_bn", [TOK, 6])
        x_mv = sb("x_mv", [TOK, 2])
        x_std = sb("x_std", [TOK, 2])
        x_r = sb("x_r", [TOK, 2])
        xl = sb("xl", [TOK, D])
        xl_bo = sb("xl_bo", [TOK, D])
        x_b2 = sb("x_b2", [TOK, D])
        xq = sb("xq", [TOK, D])
        xqT = sb("xqT", [P, TOK])
        q_sq = sb("q_sq", [TOK, INNER])
        q_n2 = sb("q_n2", [TOK, 2, XH // 2])
        q_nrm = sb("q_nrm", [TOK, 2, XH // 2])
        q_rinv = sb("q_rinv", [TOK, 2, XH // 2])
        qn = sb("qn", [TOK, INNER])
        qnT = sb("qnT", [P, PAIRS, TOK])
        w1_g = sb("w1_g", [P, MLP])
        fc1_d = sb("fc1_d", [P, MLP])
        fc1_f = sb("fc1_f", [P, MLP])
        fc1_g = sb("fc1_g", [P, MLP])
        fc2_f = sb("fc2_f", [P, MC, D])
        fc2_d = sb("fc2_d", [P, MC, D])
        bias_c = sb("bias_c", [P, 2 * MC])
        biasT = sb("biasT", [2 * MC, P])
        decay = sb("decay", [P, TOK])
        decay_heads = sb("decay_heads", [P, 8, TOK])
        half_neg = sb("half_neg", [TOK, 2])
        warm = sb("warm", [TOK, 2])
        eps_tile = sb("eps_tile", [P, 2])
        zeros = sb("zeros", [P, HALF], mybir.dt.bfloat16)
        ones_row = sb("ones_row", [1, P])
        gT = sb("gT", [P, INNER])
        m_bd = sb("m_bd", [P, PAIRS, P])
        oT = sb("oT", [P, PAIRS, TOK])
        x1 = sb("x1", [TOK, D])
        x1_r = sb("x1_r", [TOK, D])
        t_bn = sb("t_bn", [TOK, 3, 6])
        t_mv = sb("t_mv", [TOK, 3, 2])
        t_ve = sb("t_ve", [TOK, 3, 2])
        t_r = sb("t_r", [TOK, 3, 2])
        t_hat = sb("t_hat", [TOK, 3, D])
        hatT = sb("hatT", [P, 3, P])
        h1 = sb("h1", [P, MC * TOK])
        x2 = sb("x2", [TOK, D])
        x2_r = sb("x2_r", [TOK, D])
        q_heads = sb("q_heads", [P, ROWG, TOK])
        k_groups = sb("k_groups", [P, ROWG, TOK])
        v_bd = sb("v_bd", [P, D])
        scores = sb("scores", [P, 8, TOK])
        a_heads = sb("a_heads", [P, 8, TOK])
        a_outT = sb("a_outT", [P, TOK])
        x3 = sb("x3", [TOK, D])
        u = sb("u", [TOK, D])
        x3_u = sb("x3_u", [TOK, D])
        fb_half = sb("fb_half", [TOK, D])
        x3_r = sb("x3_r", [TOK, D])
        h2 = sb("h2", [P, MC * TOK])
        y_out = sb("y_out", [TOK, D])
        ps = ctx.enter_context(nc.psum_tensor("ps", [P, 8, 512], F32))
        g_ps = ps[:, 0:2, :]
        k_ps = [ps[:, 2:4, :], ps[:, 4:6, :]]
        zT_ps = ps[:, 6, :]
        misc = ps[:, 7, :]

        in_small = sem("in_small")
        in_x = sem("in_x")
        in_wk = sem("in_wk")
        in_wq = sem("in_wq")
        in_wv = sem("in_wv")
        in_row = sem("in_row")
        in_pool_w = sem("in_pool_w")
        in_tail_w = sem("in_tail_w")
        ctx_in = [sem("ctx_in0"), sem("ctx_in1"), sem("ctx_in_lead")]
        var_ready = sem("var_ready")
        std_ready = sem("std_ready")
        bn_ready = sem("bn_ready")
        r_ready = sem("r_ready")
        mr_ready = sem("mr_ready")
        zc_ready = sem("zc_ready")
        z_ready = sem("z_ready")
        zT_ready = sem("zT_ready")
        hi_ready = sem("hi_ready")
        lo_ready = sem("lo_ready")
        k_ready = sem("k_ready")
        sq_ready = sem("sq_ready")
        n2_ready = sem("n2_ready")
        nrm_ready = sem("nrm_ready")
        rinv_ready = sem("rinv_ready")
        kn_ready = sem("kn_ready")
        g_added = sem("g_added")
        fold_ready = sem("fold_ready")
        wkf_ready = sem("wkf_ready")
        wk_hi_ready = sem("wk_hi_ready")
        wk_lo_ready = sem("wk_lo_ready")
        wvf_ready = sem("wvf_ready")
        wv_ready = sem("wv_ready")
        x_stat = sem("x_stat")
        x_std_ready = sem("x_std_ready")
        xq_ready = sem("xq_ready")
        xqT_ps = sem("xqT_ps")
        xqT_ready = sem("xqT_ready")
        q_ready = sem("q_ready")
        q_sq_ready = sem("q_sq_ready")
        q_n2_ready = sem("q_n2_ready")
        q_nrm_ready = sem("q_nrm_ready")
        q_step = sem("q_step")
        qn_ready = sem("qn_ready")
        qnT_ps = sem("qnT_ps")
        qnT_ready = sem("qnT_ready")
        res_ready = sem("res_ready")
        pool_step = sem("pool_step")
        w1g_ready = sem("w1g_ready")
        fc1_ready = sem("fc1_ready")
        fc2_ready = sem("fc2_ready")
        decay_ready = sem("decay_ready")
        zero_ready = sem("zero_ready")
        eps_ready = sem("eps_ready")
        warm_done = sem("warm_done")
        bias_ps = sem("bias_ps")
        bias_col = sem("bias_col")
        biasT_ps = sem("biasT_ps")
        biasT_ready = sem("biasT_ready")
        gT_ready = sem("gT_ready")
        m_ready = sem("m_ready")
        gT_hi_ready = sem("gT_hi_ready")
        mbd_lo_ready = sem("mbd_lo_ready")
        mbd_hi_ready = sem("mbd_hi_ready")
        oT_hi_ready = sem("oT_hi_ready")
        oT_ps = sem("oT_ps")
        oT_ready = sem("oT_ready")
        y1_ready = sem("y1_ready")
        x_ready = sem("x_ready")
        tbn_ready = sem("tbn_ready")
        tmv_ready = sem("tmv_ready")
        ve_ready = sem("ve_ready")
        tr_ready = sem("tr_ready")
        hat_ready = sem("hat_ready")
        hatT_ps = sem("hatT_ps")
        hatT_ready = sem("hatT_ready")
        h1_ps = sem("h1_ps")
        h1_ready = sem("h1_ready")
        y2_ready = sem("y2_ready")
        rest_ready = sem("rest_ready")
        u_ready = sem("u_ready")
        qkv_ps = sem("qkv_ps")
        qk_ready = sem("qk_ready")
        v_ready = sem("v_ready")
        s_ps = sem("s_ps")
        s_ready = sem("s_ready")
        ao_ps = sem("ao_ps")
        ao_ready = sem("ao_ready")
        aoT_ready = sem("aoT_ready")
        y3_ready = sem("y3_ready")
        h2_ps = sem("h2_ps")
        h2_ready = sem("h2_ready")
        y4_ready = sem("y4_ready")
        final_ready = sem("final_ready")
        stored = sem("stored")

        ctx_v = ctx_rows.rearrange("(p t) d -> p t d", t=TILES)
        heads = lambda ap: ap.rearrange("p (h d) -> p h d", h=XH)

        def where(s_in_body):
            return (s_in_body // GROUP) % 2, s_in_body % GROUP

        block = ctx.enter_context(nc.Block())

        @block.sync
        def _(sp):
            sp.dma_start(cst_col[:, :], cols_consts).then_inc(in_small, 16)
            sp.dma_start(ctx_s[:, 2, 0:1, :], ctx_v[:, 0:1, :]).then_inc(ctx_in[2], 16)
            for g in range(2):
                sp.dma_start(ctx_s[:, g, :, :], ctx_v[:, 1 + GROUP * g:1 + GROUP * (g + 1), :]).then_inc(ctx_in[g], 16)
            sp.dma_start(w1_s[:, :], w1).then_inc(in_pool_w, 16)
            sp.dma_start(fc1_q[:, :], fc1).then_inc(in_pool_w, 16)
            sp.dma_start(fc2_q[:, :, :], fc2.rearrange("(c p) n -> p c n", c=MC)).then_inc(in_pool_w, 16)
            sp.dma_start(sel[:, :], chunk_select).then_inc(in_tail_w, 16)
            sp.dma_start(wv_s[:, :], wv).then_inc(in_wv, 16)
            sp.dma_start(wo_s[:, :, :], wo.rearrange("(c p) n -> p c n", c=PAIRS)).then_inc(in_tail_w, 16)
            sp.dma_start(w2_s[:, :, :], w2.rearrange("(c p) n -> p c n", c=MC)).then_inc(in_tail_w, 16)
            for n, w in enumerate((wqT, wkT, wvT, woT)):
                sp.dma_start(attn_w[:, n, :], w).then_inc(in_tail_w, 16)
            with sp.Fori(0, ITERS - 1) as i:
                for g in range(2):
                    sp.wait_ge(z_ready, i * BODY + 1 + GROUP * (g + 1))
                    first = i * BODY + 1 + GROUP * (2 + g)
                    sp.dma_start(ctx_s[:, g, :, :], ctx_v[:, bass.ds(first, GROUP), :]).then_inc(ctx_in[g], 16)
            sp.wait_ge(final_ready, 1)
            sp.dma_start(out, y_out[:, :]).then_inc(stored, 16)
            sp.wait_ge(stored, 16)

        @block.gpsimd
        def _(pool):
            nc.gpsimd.memset(half_neg[:, :], -0.5).then_inc(pool_step, 1)
            nc.gpsimd.memset(m_bd[:, :, :], 0.0).then_inc(zero_ready, 1)
            nc.gpsimd.memset(ones_row[:, :], 1.0).then_inc(zero_ready, 1)
            nc.gpsimd.memset(v_bd[:, :], 0.0).then_inc(zero_ready, 1)
            pool.wait_ge(in_wk, 16)
            pool.dma_start(row[:, :], rows.partition_broadcast(P)).then_inc(in_row, 16)
            pool.wait_ge(in_small, 16)
            pool.wait_ge(in_pool_w, 48)
            pool.wait_ge(in_row, 16)
            nc.gpsimd.tensor_scalar(w1_g[:, :], w1_s[:, :], col[:, 2:3], 0.0, ALU.mult, ALU.add).then_inc(w1g_ready, 1)
            nc.gpsimd.tensor_scalar(fc1_f[:, :], fc1_q[:, :], -128.0, 1.0, ALU.add, ALU.mult).then_inc(pool_step, 1)
            nc.gpsimd.tensor_scalar(fc2_f[:, :, :], fc2_q[:, :, :], -128.0, 1.0, ALU.add, ALU.mult).then_inc(pool_step, 1)
            pool.wait_ge(pool_step, 2)
            nc.gpsimd.tensor_tensor(fc1_d[:, :], fc1_f[:, :], row[:, R_S1:R_S1 + MLP], ALU.mult).then_inc(pool_step, 1)
            pool.wait_ge(pool_step, 3)
            nc.gpsimd.tensor_tensor(fc2_d[:, :, :], fc2_f[:, :, :],
                                    row[:, R_S2:R_S2 + MLP].rearrange("p (c n) -> p c n", c=MC),
                                    ALU.mult).then_inc(fc2_ready, 1)
            pool.wait_ge(pool_step, 4)
            nc.gpsimd.tensor_scalar(fc1_g[:, :], fc1_d[:, :], col[:, 4:5], 0.0, ALU.mult, ALU.add).then_inc(fc1_ready, 1)
            nc.gpsimd.tensor_tensor(decay[:, :], col[:, C_GAM:C_GAM + 1].broadcast_to([P, TOK]),
                                    cst[:, C_IDX:C_IDX + TOK], ALU.pow).then_inc(pool_step, 1)
            pool.wait_ge(pool_step, 5)
            nc.gpsimd.tensor_tensor(decay_heads[:, :, :], decay[:, :].unsqueeze(1).broadcast_to([P, 8, TOK]),
                                    cst[:, C_H8:C_H8 + 8].unsqueeze(2).broadcast_to([P, 8, TOK]),
                                    ALU.mult).then_inc(decay_ready, 1)
            for n in range(3):
                w = 2 if n == 2 else 1
                pool.wait_ge(ve_ready, (1, 2, 4)[n])
                nc.gpsimd.tensor_tensor(t_r[:, n, 0:w], t_ve[:, n, 0:w], half_neg[:, 0:w], ALU.pow).then_inc(tr_ready, 1)

        @block.scalar
        def _(act):
            act.dma_start(wk_s[:, :], wk).then_inc(in_wk, 16)
            act.wait_ge(eps_ready, 2)
            nc.scalar.activation(warm[:, 0:1], eps_tile[0:TOK, 0:1], ACT.Sqrt).then_inc(warm_done, 1)
            act.dma_start(xs[:, :], x).then_inc(in_x, 16)
            act.dma_start(wq_s[:, :], wq).then_inc(in_wq, 16)

            def group_std(slot, count, group):
                act.wait_ge(var_ready, group + 2)
                nc.scalar.activation(ln_std[:, slot, 0:count], mv[:, slot, 0:count, 1], ACT.Sqrt, bias=eps_c(0),
                                     scale=1.0).then_inc(std_ready, 1)

            def z_high(slot, count, group):
                act.wait_ge(zT_ready, group + 2)
                nc.scalar.activation(zT_hi[:, slot, 0:count * P], zT_ps[:, 0:count * P],
                                     ACT.Copy).then_inc(hi_ready, 1)

            def make_z(slot, places, group):
                act.wait_ge(zc_ready, group + 2)
                for j in places:
                    if not (type(group) is int and group < 2):
                        act.wait_ge(g_added, group * GROUP + (j + 2 - 2 * GROUP))
                    nc.scalar.activation(z[:, slot, j, :], ctx_s[:, slot, j, :], ACT.Identity,
                                         bias=ln_c[:, slot, j:j + 1], scale=ln_r[:, slot, j:j + 1]).then_inc(z_ready, 1)

            def square(s, buf):
                act.wait_ge(k_ready, s + 1)
                if not (type(s) is int and s < 2):
                    act.wait_ge(n2_ready, s - 1)
                nc.scalar.activation(k_sq[:, buf, :], k_ps[buf], ACT.Square).then_inc(sq_ready, 1)

            def norm(s, buf):
                act.wait_ge(n2_ready, s + 1)
                nc.scalar.activation(nrm[:, buf, :], n2[:, buf, :], ACT.Sqrt).then_inc(nrm_ready, 1)

            def eps_c(n, p=P):
                return eps_tile[0:p, n:n + 1]

            def query_extra(j):
                half = j // 4
                c = slice(half * HALF, (half + 1) * HALF)
                if j in (1, 4):
                    act.wait_ge(q_ready, half + 1)
                    nc.scalar.activation(q_sq[:, c], misc[0:TOK, :], ACT.Square).then_inc(q_sq_ready, 1)
                elif j in (2, 5):
                    act.wait_ge(q_n2_ready, half + 1)
                    nc.scalar.activation(q_nrm[:, half, :], q_n2[:, half, :], ACT.Sqrt).then_inc(q_nrm_ready, 1)
                elif j in (3, 6):
                    act.wait_ge(qnT_ps, half + 1)
                    nc.scalar.activation(qnT[:, 4 * half:4 * half + 4, :], misc[:, 0:4 * TOK].rearrange(
                        "p (c t) -> p c t", t=TOK), ACT.Copy).then_inc(qnT_ready, 1)

            def weight_extra(j):
                if j < 2:
                    act.wait_ge(wvf_ready, j + 1)
                    nc.scalar.activation(wv_f[:, j * HALF:(j + 1) * HALF], misc, ACT.Copy).then_inc(wv_ready, 1)

            group_std(2, 1, -1)
            make_z(2, range(1), -1)
            group_std(0, GROUP, 0)
            for half in range(2):
                act.wait_ge(wkf_ready, half + 1)
                nc.scalar.activation(wk_hi[:, half * HALF:(half + 1) * HALF], k_ps[0][:, half, :],
                                     ACT.Copy).then_inc(wk_hi_ready, 1)
                if half == 0:
                    z_high(2, 1, -1)
            make_z(0, range(GROUP), 0)
            z_high(0, GROUP, 0)
            square(0, 0)
            act.wait_ge(x_stat, 2)
            nc.scalar.activation(x_std[:, 0:1], x_mv[:, 1:2], ACT.Sqrt, bias=eps_c(0, TOK),
                                 scale=1.0).then_inc(x_std_ready, 1)
            nc.scalar.activation(x_std[:, 1:2], x_mv[:, 1:2], ACT.Sqrt, bias=eps_c(1, TOK),
                                 scale=1.0 + EPS).then_inc(x_std_ready, 1)
            norm(0, 0)

            def body(i, first=False, last=False):
                for j in range(BODY):
                    s = i * BODY + (1 + j)
                    slot, place = where(j + GROUP)
                    group = i * 2 + (j // GROUP + 1)
                    prepare = not (last and j >= GROUP)
                    if place == 1 and prepare:
                        group_std(slot, GROUP, group)
                    square(s, (1 + j) % 2)
                    if place == 2 and prepare:
                        z_high(slot, GROUP, group)
                    if place == 1 and prepare:
                        make_z(slot, range(2), group)
                    norm(s, (1 + j) % KN)
                    if place == 1 and prepare:
                        make_z(slot, range(2, GROUP), group)
                    if first:
                        query_extra(j)
                    if last:
                        weight_extra(j)

            body(0, first=True)
            with act.Fori(1, ITERS - 1) as i:
                body(i)
            body(ITERS - 1, last=True)
            act.wait_ge(pool_step, 1)
            act.wait_ge(warm_done, 1)
            nc.scalar.activation(warm[:, 0:1], half_neg[:, 0:1], ACT.Gelu).then_inc(warm_done, 1)
            act.wait_ge(g_added, TILES)
            nc.scalar.activation(gT[:, 0:HALF], ps[:, 0, :], ACT.Copy).then_inc(gT_ready, 1)
            act.wait_ge(zero_ready, 1)
            for half in range(2):
                act.wait_ge(m_ready, half + 1)
                nc.scalar.activation(m_bd[0:XD, 4 * half:4 * half + 4, 0:XD],
                                     ps[0:XD, 2 + half, :].rearrange("p (c n) -> p c n", n=P)[:, :, 0:XD],
                                     ACT.Copy).then_inc(mbd_lo_ready, 1)
            act.wait_ge(oT_ps, 1)
            nc.scalar.activation(oT[:, 0:PAIRS // 2, :], ps[:, 4, 0:256], ACT.Copy).then_inc(oT_ready, 1)
            act.wait_ge(h1_ps, 1)
            nc.scalar.activation(h1[:, :], ps[:, 7, 0:MC * TOK], ACT.Gelu).then_inc(h1_ready, 1)
            act.wait_ge(warm_done, 2)
            nc.scalar.activation(warm[:, 1:2], half_neg[:, 0:1], ACT.Silu).then_inc(warm_done, 1)
            act.wait_ge(qkv_ps, 3)
            act.wait_ge(zero_ready, 3)
            for half in range(2):
                at = 64 * half
                nc.scalar.activation(v_bd[at:at + 64, at:at + 64], ps[at:at + 64, 1, 256 + at:320 + at],
                                     ACT.Copy).then_inc(v_ready, 1)
            act.wait_ge(h2_ps, 1)
            nc.scalar.activation(h2[:, :], ps[:, 7, 0:MC * TOK], ACT.Silu).then_inc(h2_ready, 1)

        @block.vector
        def _(dve):
            def stats(slot, places):
                for j in places:
                    last = nc.vector.bn_stats(bn[:, slot, j, :], ctx_s[:, slot, j, :])
                last.then_inc(bn_ready, 1)

            def aggregate(slot, count):
                for j in range(count):
                    last = nc.vector.bn_aggr(mv[:, slot, j, :], bn[:, slot, j, :])
                last.then_inc(var_ready, 1)

            def z_scalars(slot, count, group):
                dve.wait_ge(std_ready, group + 2)
                nc.vector.reciprocal(ln_r[:, slot, 0:count], ln_std[:, slot, 0:count]).then_inc(r_ready, 1)
                dve.wait_ge(r_ready, group + 2)
                nc.vector.tensor_tensor(ln_mr[:, slot, 0:count], mv[:, slot, 0:count, 0], ln_r[:, slot, 0:count],
                                        ALU.mult).then_inc(mr_ready, 1)
                dve.wait_ge(mr_ready, group + 2)
                nc.vector.tensor_scalar(ln_c[:, slot, 0:count], ln_mr[:, slot, 0:count], -1.0, 1.0,
                                        ALU.mult, ALU.add).then_inc(zc_ready, 1)

            def z_low(slot, count, group):
                dve.wait_ge(hi_ready, group + 2)
                nc.vector.tensor_tensor(zT_lo[:, slot, 0:count * P], zT_ps[:, 0:count * P],
                                        zT_hi[:, slot, 0:count * P].bitcast(F32), ALU.subtract).then_inc(lo_ready, 1)

            def head_sums(s, sq, buf):
                dve.wait_ge(sq_ready, s + 1)
                nc.vector.tensor_reduce(n2[:, buf, :], heads(k_sq[:, sq, :]), AX_X, ALU.add).then_inc(n2_ready, 1)

            def normalise(s, kbuf, buf, stats_of=None):
                if stats_of is not None:
                    dve.wait_ge(bn_ready, stats_of * 2 + 3)
                dve.wait_ge(nrm_ready, s + 1)
                nc.vector.reciprocal(rinv[:, buf, :], nrm[:, buf, :]).then_inc(rinv_ready, 1)
                dve.wait_ge(rinv_ready, s + 1)
                if not (type(s) is int and s < KN):
                    dve.wait_ge(g_added, s - KN + 1)
                nc.vector.scalar_tensor_tensor(
                    heads(kn[:, buf, :]),
                    rinv[:, buf, :].unsqueeze(2).broadcast_to([P, XH, XD]), 1.0 / TINY,
                    k_ps[kbuf].rearrange("p b (h d) -> p (b h) d", d=XD),
                    ALU.min, ALU.mult).then_inc(kn_ready, 1)

            nc.vector.memset(eps_tile[:, 0:1], EPS).then_inc(eps_ready, 1)
            nc.vector.memset(eps_tile[:, 1:2], EPS * EPS).then_inc(eps_ready, 1)
            nc.vector.memset(zeros[:, :], 0.0).then_inc(eps_ready, 1)
            dve.wait_ge(in_small, 16)
            nc.vector.tensor_tensor(fold_d[:, 0:1], col[:, 1:2], col[:, 0:1], ALU.subtract).then_inc(fold_ready, 1)
            dve.wait_ge(fold_ready, 1)
            nc.vector.tensor_scalar(fold_d[:, 1:2], fold_d[:, 0:1], 1.0 / D, None, ALU.mult).then_inc(fold_ready, 1)
            dve.wait_ge(fold_ready, 2)
            nc.vector.tensor_scalar(fold[:, :], ident, col[:, 0:1], fold_d[:, 1:2], ALU.mult, ALU.add).then_inc(fold_ready, 1)
            dve.wait_ge(ctx_in[2], 16)
            stats(2, range(1))
            dve.wait_ge(bn_ready, 1)
            aggregate(2, 1)
            z_scalars(2, 1, -1)
            dve.wait_ge(ctx_in[0], 16)
            stats(0, range(2))
            stats(0, range(2, GROUP))
            dve.wait_ge(bn_ready, 3)
            aggregate(0, GROUP)
            z_scalars(0, GROUP, 0)
            for half in range(2):
                dve.wait_ge(wk_hi_ready, half + 1)
                nc.vector.tensor_tensor(wk_lo[:, half * HALF:(half + 1) * HALF], k_ps[0][:, half, :],
                                        wk_hi[:, half * HALF:(half + 1) * HALF].bitcast(F32),
                                        ALU.subtract).then_inc(wk_lo_ready, 1)
                if half == 0:
                    z_low(2, 1, -1)
            dve.wait_ge(in_x, 16)
            nc.vector.bn_stats(x_bn[:, :], xs[:, :]).then_inc(x_stat, 1)
            dve.wait_ge(x_stat, 1)
            nc.vector.bn_aggr(x_mv[:, :], x_bn[:, :]).then_inc(x_stat, 1)
            z_low(0, GROUP, 0)
            head_sums(0, 0, 0)
            dve.wait_ge(x_std_ready, 2)
            nc.vector.reciprocal(x_r[:, :], x_std[:, :]).then_inc(x_stat, 1)
            dve.wait_ge(x_stat, 3)
            nc.vector.tensor_scalar(xq[:, :], xs[:, :], x_mv[:, 0:1], x_r[:, 1:2], ALU.subtract, ALU.mult).then_inc(xq_ready, 1)
            normalise(0, 0, 0)
            nc.vector.tensor_scalar(xl[:, :], xs[:, :], x_mv[:, 0:1], x_r[:, 0:1], ALU.subtract, ALU.mult).then_inc(x_stat, 1)
            dve.wait_ge(ctx_in[1], 16)
            stats(1, range(2))
            stats(1, range(2, GROUP))
            dve.wait_ge(bn_ready, 5)

            def query_extra(j):
                half = j // 4
                c = slice(half * HALF, (half + 1) * HALF)
                if j == 0:
                    dve.wait_ge(xqT_ps, 1)
                    nc.vector.tensor_scalar(xqT[:, :], misc[:, 0:TOK], col[:, 0:1], col[:, 1:2], ALU.mult,
                                            ALU.add).then_inc(xqT_ready, 1)
                elif j in (1, 4):
                    dve.wait_ge(q_sq_ready, half + 1)
                    nc.vector.tensor_reduce(q_n2[:, half, :], q_sq[:, c].rearrange("p (h d) -> p h d", d=XD), AX_X,
                                            ALU.add).then_inc(q_n2_ready, 1)
                elif j in (2, 5):
                    dve.wait_ge(q_nrm_ready, half + 1)
                    nc.vector.reciprocal(q_rinv[:, half, :], q_nrm[:, half, :]).then_inc(q_step, 1)
                    dve.wait_ge(q_step, half + 1)
                    nc.vector.scalar_tensor_tensor(
                        qn[:, c].rearrange("p (h d) -> p h d", d=XD),
                        q_rinv[:, half, :].unsqueeze(2).broadcast_to([TOK, XH // 2, XD]), 1.0 / TINY,
                        misc[0:TOK, :].rearrange("p (h d) -> p h d", d=XD), ALU.min, ALU.mult).then_inc(qn_ready, 1)

            def weight_extra(j):
                if j == 2:
                    dve.wait_ge(bias_ps, 1)
                    nc.vector.tensor_tensor(bias_c[:, :], misc[:, 0:2 * MC], col[:, C_B1:C_B1 + 2 * MC],
                                            ALU.add).then_inc(bias_col, 1)
                elif j == 4:
                    dve.wait_ge(biasT_ps, 1)
                    nc.vector.tensor_copy(biasT[:, :], misc[0:2 * MC, 0:P]).then_inc(biasT_ready, 1)
                elif j == 5:
                    dve.wait_ge(in_row, 16)
                    nc.vector.tensor_tensor(xl_bo[:, :], xl[:, :], row[0:TOK, R_BO:R_BO + D], ALU.add).then_inc(res_ready, 1)
                    nc.vector.tensor_tensor(x_b2[:, :], xs[:, :], row[0:TOK, R_B2:R_B2 + D], ALU.add).then_inc(res_ready, 1)
                    nc.vector.tensor_scalar(fb_half[:, :], row[0:TOK, R_FB2:R_FB2 + D], 0.5, None,
                                            ALU.mult).then_inc(res_ready, 1)

            def body(i, first=False, last=False):
                for j in range(BODY):
                    s = i * BODY + (1 + j)
                    slot, place = where(j + GROUP)
                    group = i * 2 + (j // GROUP + 1)
                    prepare = not (last and j >= GROUP)
                    if place == 1 and prepare:
                        z_scalars(slot, GROUP, group)
                    head_sums(s, (1 + j) % 2, (1 + j) % KN)
                    if place == 0 and prepare:
                        aggregate(slot, GROUP)
                    if place == 1 and not last:
                        dve.wait_ge(ctx_in[1 - slot], i * 16 + 32)
                        stats(1 - slot, range(2))
                    if place == 2 and prepare:
                        z_low(slot, GROUP, group)
                    if place == 3 and not last:
                        stats(1 - slot, range(2, GROUP))
                    normalise(s, (1 + j) % 2, (1 + j) % KN, group + 1 if place == 3 and not last else None)
                    if first:
                        query_extra(j)
                    if last:
                        weight_extra(j)

            body(0, first=True)
            with dve.Fori(1, ITERS - 1) as i:
                body(i)
            body(ITERS - 1, last=True)

            def layernorm(n, src):
                dve.wait_ge(x_ready, n + 1)
                nc.vector.bn_stats(t_bn[:, n, :], src).then_inc(tbn_ready, 1)
                dve.wait_ge(tbn_ready, n + 1)
                nc.vector.bn_aggr(t_mv[:, n, :], t_bn[:, n, :]).then_inc(tmv_ready, 1)
                dve.wait_ge(tmv_ready, n + 1)
                nc.vector.tensor_scalar(t_ve[:, n, 0:1], t_mv[:, n, 1:2], EPS, None, ALU.add).then_inc(ve_ready, 1)
                if n == 2:
                    nc.vector.tensor_scalar(t_ve[:, n, 1:2], t_mv[:, n, 1:2], 1.0 + EPS, EPS * EPS,
                                            ALU.mult, ALU.add).then_inc(ve_ready, 1)
                dve.wait_ge(tr_ready, n + 1)
                which = 1 if n == 2 else 0
                nc.vector.tensor_scalar(t_hat[:, n, :], src, t_mv[:, n, 0:1], t_r[:, n, which:which + 1],
                                        ALU.subtract, ALU.mult).then_inc(hat_ready, 1)

            dve.wait_ge(g_added, TILES)
            nc.vector.tensor_copy(gT[:, HALF:INNER], ps[:, 1, :]).then_inc(gT_hi_ready, 1)
            dve.wait_ge(zero_ready, 1)
            for half in range(2):
                dve.wait_ge(m_ready, half + 1)
                nc.vector.tensor_copy(m_bd[XD:P, 4 * half:4 * half + 4, XD:P],
                                      ps[XD:P, 2 + half, :].rearrange("p (c n) -> p c n", n=P)[:, :, XD:P]
                                      ).then_inc(mbd_hi_ready, 1)
            dve.wait_ge(oT_ps, 2)
            nc.vector.tensor_copy(oT[:, PAIRS // 2:PAIRS, :], ps[:, 5, 0:256].rearrange("p (c t) -> p c t", t=TOK)
                                  ).then_inc(oT_hi_ready, 1)
            dve.wait_ge(y1_ready, 1)
            dve.wait_ge(res_ready, 3)
            nc.vector.tensor_tensor(x1[:, :], ps[0:TOK, 6, 0:D], xl_bo[:, :], ALU.add).then_inc(x_ready, 1)
            layernorm(0, x1[:, :])
            nc.vector.tensor_tensor(x1_r[:, :], x1[:, :], x_b2[:, :], ALU.add).then_inc(rest_ready, 1)
            dve.wait_ge(hatT_ps, 1)
            nc.vector.tensor_copy(hatT[:, 0, 0:TOK], ps[:, 6, 0:TOK]).then_inc(hatT_ready, 1)
            dve.wait_ge(y2_ready, 1)
            dve.wait_ge(rest_ready, 1)
            nc.vector.tensor_tensor(x2[:, :], ps[0:TOK, 0, 0:D], x1_r[:, :], ALU.add).then_inc(x_ready, 1)
            layernorm(1, x2[:, :])
            nc.vector.tensor_tensor(x2_r[:, :], x2[:, :], row[0:TOK, R_ABO:R_ABO + D], ALU.add).then_inc(rest_ready, 1)
            dve.wait_ge(hatT_ps, 2)
            nc.vector.tensor_copy(hatT[:, 1, :].rearrange("p (a t) -> p a t", a=2),
                                  ps[:, 6, 0:TOK].unsqueeze(1).broadcast_to([P, 2, TOK])).then_inc(hatT_ready, 1)
            dve.wait_ge(qkv_ps, 1)
            nc.vector.scalar_tensor_tensor(
                q_heads[:, :, :], ps[:, 7, 0:TOK].unsqueeze(1).broadcast_to([P, ROWG, TOK]), col[:, 6:7],
                cst[:, C_HEAD:C_HEAD + ROWG].unsqueeze(2).broadcast_to([P, ROWG, TOK]),
                ALU.add, ALU.mult).then_inc(qk_ready, 1)
            dve.wait_ge(qkv_ps, 2)
            nc.vector.scalar_tensor_tensor(
                k_groups[:, :, :], ps[:, 5, 0:TOK].unsqueeze(1).broadcast_to([P, ROWG, TOK]), col[:, 7:8],
                cst[:, C_GRP:C_GRP + ROWG].unsqueeze(2).broadcast_to([P, ROWG, TOK]),
                ALU.add, ALU.mult).then_inc(qk_ready, 1)
            dve.wait_ge(s_ps, 1)
            nc.vector.tensor_tensor(scores[:, :, :], ps[:, 2, :].rearrange("p (c t) -> p c t", t=TOK),
                                    cst[:, C_CAUSAL:C_CAUSAL + TOK].unsqueeze(1).broadcast_to([P, 8, TOK]),
                                    ALU.mult).then_inc(s_ready, 1)
            dve.wait_ge(ao_ps, 1)
            dve.wait_ge(decay_ready, 1)
            nc.vector.tensor_tensor(a_heads[:, :, :], ps[:, 3, :].rearrange("p (c t) -> p c t", t=TOK),
                                    decay_heads[:, :, :], ALU.mult).then_inc(ao_ready, 1)
            dve.wait_ge(ao_ready, 1)
            nc.vector.tensor_reduce(a_outT[:, :], a_heads[:, :, :].rearrange("p c t -> p t c"), AX_X,
                                    ALU.add).then_inc(aoT_ready, 1)
            dve.wait_ge(y3_ready, 1)
            dve.wait_ge(rest_ready, 2)
            nc.vector.tensor_tensor(x3[:, :], ps[0:TOK, 0, 0:D], x2_r[:, :], ALU.add).then_inc(x_ready, 1)
            layernorm(2, x3[:, :])
            nc.vector.tensor_scalar(u[:, :], x3[:, :], t_mv[:, 2, 0:1], t_r[:, 2, 0:1],
                                    ALU.subtract, ALU.mult).then_inc(u_ready, 1)
            dve.wait_ge(hatT_ps, 3)
            nc.vector.tensor_copy(hatT[:, 2, 0:TOK], ps[:, 6, 0:TOK]).then_inc(hatT_ready, 1)
            dve.wait_ge(u_ready, 1)
            nc.vector.tensor_tensor(x3_u[:, :], x3[:, :], u[:, :], ALU.add).then_inc(u_ready, 1)
            dve.wait_ge(u_ready, 2)
            nc.vector.tensor_tensor(x3_r[:, :], x3_u[:, :], fb_half[:, :], ALU.add).then_inc(rest_ready, 1)
            dve.wait_ge(y4_ready, 1)
            dve.wait_ge(rest_ready, 3)
            nc.vector.scalar_tensor_tensor(y_out[:, :], ps[0:TOK, 1, 0:D], 0.5, x3_r[:, :],
                                           ALU.mult, ALU.add).then_inc(final_ready, 1)

        @block.tensor
        def _(pe):
            mm = nc.tensor.matmul

            def transposes(slot, count, group):
                pe.wait_ge(z_ready, GROUP * group + (GROUP + 1))
                for j in range(count):
                    last = nc.tensor.transpose(zT_ps[:, j * P:(j + 1) * P], z[:, slot, j, :], ident)
                last.then_inc(zT_ready, 1)

            def keys(s, buf, slot, place, group, lead=False):
                if place == 0:
                    pe.wait_ge(hi_ready, group + 2)
                    pe.wait_ge(lo_ready, group + 2)
                if not (type(s) is int and s < 2):
                    pe.wait_ge(kn_ready, s - 1)
                hi = zT_hi[:, slot, place * P:(place + 1) * P]
                lo = zT_lo[:, slot, place * P:(place + 1) * P]
                for half in range(2):
                    if lead:
                        pe.wait_ge(wk_lo_ready, half + 1)
                    c = slice(half * HALF, (half + 1) * HALF)
                    o = k_ps[buf][:, half, :]
                    mm(o, hi, wk_lo[:, c], start=True, stop=False)
                    mm(o, lo, wk_hi[:, c], start=False, stop=False)
                    last = mm(o, hi, wk_hi[:, c], start=False, stop=True)
                last.then_inc(k_ready, 1)

            def add_g(s, buf, slot, place, first=False, final=False):
                pe.wait_ge(kn_ready, s + 1)
                for half in range(2):
                    last = mm(g_ps[:, half, :], z[:, slot, place, :], kn[:, buf, half * HALF:(half + 1) * HALF],
                              start=first, stop=final)
                last.then_inc(g_added, 1)

            pe.wait_ge(eps_ready, 3)
            for _ in range(WARM):
                mm(misc, zeros[:, 0:P], zeros[:, :], start=True, stop=True)
            pe.wait_ge(fold_ready, 3)
            pe.wait_ge(in_wk, 16)
            for half in range(2):
                mm(k_ps[0][:, half, :], fold[:, :], wk_s[:, half * HALF:(half + 1) * HALF], start=True,
                   stop=True).then_inc(wkf_ready, 1)
            transposes(2, 1, -1)
            keys(0, 0, 2, 0, -1, lead=True)
            transposes(0, GROUP, 0)
            def query_extra(j):
                half = j // 4
                if j == 0:
                    pe.wait_ge(xq_ready, 1)
                    nc.tensor.transpose(misc[:, 0:TOK], xq[:, :], ident[0:TOK, 0:TOK]).then_inc(xqT_ps, 1)
                elif j in (1, 4):
                    if half == 0:
                        pe.wait_ge(xqT_ready, 1)
                        pe.wait_ge(in_wq, 16)
                    else:
                        pe.wait_ge(qnT_ready, 1)
                    mm(misc[0:TOK, :], xqT[:, :], wq_s[:, half * HALF:(half + 1) * HALF], start=True,
                       stop=True).then_inc(q_ready, 1)
                elif j in (3, 6):
                    pe.wait_ge(qn_ready, half + 1)
                    for c in range(4):
                        at = (4 * half + c) * P
                        last = nc.tensor.transpose(misc[:, c * TOK:(c + 1) * TOK], qn[:, at:at + P], ident[0:TOK, 0:TOK])
                    last.then_inc(qnT_ps, 1)

            def weight_extra(j):
                if j < 2:
                    if j == 0:
                        pe.wait_ge(in_wv, 16)
                        pe.wait_ge(qnT_ready, 2)
                    else:
                        pe.wait_ge(wv_ready, 1)
                    mm(misc, fold[:, :], wv_s[:, j * HALF:(j + 1) * HALF], start=True, stop=True).then_inc(wvf_ready, 1)
                elif j == 2:
                    pe.wait_ge(in_pool_w, 48)
                    pe.wait_ge(fc1_ready, 1)
                    pe.wait_ge(wv_ready, 2)
                    for c in range(MC):
                        mm(misc[:, c:c + 1], w1_s[:, c * P:(c + 1) * P], col[:, 3:4], start=True, stop=True)
                    for c in range(MC):
                        last = mm(misc[:, MC + c:MC + c + 1], fc1_d[:, c * P:(c + 1) * P], col[:, 5:6], start=True, stop=True)
                    last.then_inc(bias_ps, 1)
                elif j == 4:
                    pe.wait_ge(bias_col, 1)
                    nc.tensor.transpose(misc[0:2 * MC, 0:P], bias_c[:, :], ident).then_inc(biasT_ps, 1)

            def body(i, first=False, last=False):
                for j in range(BODY):
                    s = i * BODY + (1 + j)
                    slot, place = where(j)
                    group = i * 2 + j // GROUP
                    if place == 3 and not (last and j >= GROUP):
                        transposes(where(j + GROUP)[0], GROUP, group + 1)
                    keys(s, (1 + j) % 2, slot, place, group)
                    if first and j < 2:
                        if j == 1:
                            add_g(0, 0, 2, 0, first=True)
                    else:
                        add_g(s - 2, (j - 1) % KN, *where((j - 2) % BODY))
                    if first:
                        query_extra(j)
                    if last:
                        weight_extra(j)

            body(0, first=True)
            with pe.Fori(1, ITERS - 1) as i:
                body(i)
            body(ITERS - 1, last=True)
            add_g(TILES - 2, (TILES - 2) % KN, *where(BODY - 2))
            add_g(TILES - 1, (TILES - 1) % KN, *where(BODY - 1), final=True)

            for half in range(2):
                if half == 0:
                    pe.wait_ge(gT_ready, 1)
                    pe.wait_ge(wv_ready, 2)
                else:
                    pe.wait_ge(gT_hi_ready, 1)
                for c in range(4 * half, 4 * half + 4):
                    last = mm(ps[:, 2 + half, (c % 4) * P:(c % 4 + 1) * P], gT[:, c * P:(c + 1) * P],
                              wv_f[:, c * P:(c + 1) * P], start=True, stop=True)
                last.then_inc(m_ready, 1)
            for half in range(2):
                pe.wait_ge(mbd_lo_ready, half + 1)
                pe.wait_ge(mbd_hi_ready, half + 1)
                for c in range(4 * half, 4 * half + 4):
                    last = mm(ps[:, 4 + half, (c % 4) * TOK:(c % 4 + 1) * TOK], m_bd[:, c, :], qnT[:, c, :],
                              start=True, stop=True)
                last.then_inc(oT_ps, 1)
            pe.wait_ge(in_tail_w, 16 * 7)
            for half in range(2):
                if half == 0:
                    pe.wait_ge(oT_ready, 1)
                else:
                    pe.wait_ge(oT_hi_ready, 1)
                for c in range(4 * half, 4 * half + 4):
                    last = mm(ps[0:TOK, 6, 0:D], oT[:, c, :], wo_s[:, c, :], start=(c == 0), stop=(c == PAIRS - 1))
            last.then_inc(y1_ready, 1)

            def hat_transpose(n):
                pe.wait_ge(hat_ready, n + 1)
                nc.tensor.transpose(ps[:, 6, 0:TOK], t_hat[:, n, :], ident[0:TOK, 0:TOK]).then_inc(hatT_ps, 1)

            def hidden_bias(n):
                pe.wait_ge(biasT_ready, 1)
                mm(ps[:, 7, 0:MC * TOK], biasT[:, :], sel[:, n * MC * TOK:(n + 1) * MC * TOK], start=True, stop=False,
                   skip_group_check=True)

            hidden_bias(0)
            hat_transpose(0)
            pe.wait_ge(hatT_ready, 1)
            for c in range(MC):
                last = mm(ps[:, 7, c * TOK:(c + 1) * TOK], w1_g[:, c * P:(c + 1) * P], hatT[:, 0, 0:TOK],
                          start=False, stop=(c == MC - 1), skip_group_check=True)
            last.then_inc(h1_ps, 1)
            pe.wait_ge(h1_ready, 1)
            for c in range(MC):
                last = mm(ps[0:TOK, 0, 0:D], h1[:, c * TOK:(c + 1) * TOK], w2_s[:, c, :], start=(c == 0), stop=(c == MC - 1))
            last.then_inc(y2_ready, 1)
            hat_transpose(1)
            pe.wait_ge(hatT_ready, 2)
            mm(ps[:, 7, 0:TOK], attn_w[:, 0, :], hatT[:, 1, 0:TOK], start=True, stop=True).then_inc(qkv_ps, 1)
            mm(ps[:, 5, 0:TOK], attn_w[:, 1, :], hatT[:, 1, 0:TOK], start=True, stop=True).then_inc(qkv_ps, 1)
            pe.wait_ge(in_row, 16)
            pe.wait_ge(zero_ready, 3)
            mm(ps[:, 1, 256:384], hatT[:, 1, :], attn_w[:, 2, :], start=True, stop=False)
            mm(ps[:, 1, 256:384], ones_row[0:1, :], row[0:1, R_BV:R_BV + D], start=False, stop=True).then_inc(qkv_ps, 1)
            pe.wait_ge(qk_ready, 2)
            for g in range(2):
                last = mm(ps[:, 2, 256 * g:256 * g + 256], k_groups[:, 2 * g:2 * g + 2, :],
                          q_heads[:, :, :], start=True, stop=True)
            last.then_inc(s_ps, 1)
            pe.wait_ge(s_ready, 1)
            pe.wait_ge(v_ready, 2)
            mm(ps[:, 3, :], v_bd[:, :], scores[:, :, :], start=True, stop=True).then_inc(ao_ps, 1)
            pe.wait_ge(aoT_ready, 1)
            mm(ps[0:TOK, 0, 0:D], a_outT[:, :], attn_w[:, 3, :], start=True, stop=True).then_inc(y3_ready, 1)
            hidden_bias(1)
            hat_transpose(2)
            pe.wait_ge(hatT_ready, 3)
            for c in range(MC):
                last = mm(ps[:, 7, c * TOK:(c + 1) * TOK], fc1_g[:, c * P:(c + 1) * P], hatT[:, 2, 0:TOK],
                          start=False, stop=(c == MC - 1), skip_group_check=True)
            last.then_inc(h2_ps, 1)
            pe.wait_ge(h2_ready, 1)
            pe.wait_ge(fc2_ready, 1)
            for c in range(MC):
                last = mm(ps[0:TOK, 1, 0:D], h2[:, c * TOK:(c + 1) * TOK], fc2_d[:, c, :], start=(c == 0), stop=(c == MC - 1))
            last.then_inc(y4_ready, 1)


def kernel(x, ctx_1024, L0_xattn_wq, L0_xattn_wk, L0_xattn_wv, L0_xattn_wo, L0_xattn_bo, L0_xattn_w1, L0_xattn_b1,
           L0_xattn_w2, L0_xattn_b2, L0_xattn_ln1_g, L0_xattn_ln1_b, L0_xattn_ln2_g, L0_xattn_ln2_b, L0_attn_Wq,
           L0_attn_bq, L0_attn_Wk, L0_attn_bk, L0_attn_Wv, L0_attn_bv, L0_attn_Wo, L0_attn_bo, L0_attn_gamma,
           L0_ffn_ln_gamma, L0_ffn_ln_beta, L0_ffn_fc1_q, L0_ffn_fc1_scales, L0_ffn_fc1_bias, L0_ffn_fc2_q,
           L0_ffn_fc2_scales, L0_ffn_fc2_bias):
    import numpy as np
    import concourse.bacc as bacc
    from concourse import mybir as mb
    from concourse.bass_utils import run_bass_kernel_spmd

    lay = np.ascontiguousarray
    chunks = lambda v: np.asarray(v).reshape(MC, P).T
    column = lambda v: np.asarray(v).reshape(P, 1)
    cols = np.concatenate([column(v) for v in (L0_xattn_ln1_g, L0_xattn_ln1_b, L0_xattn_ln2_g, L0_xattn_ln2_b,
                                               L0_ffn_ln_gamma, L0_ffn_ln_beta, L0_attn_bq, L0_attn_bk)]
                          + [chunks(L0_xattn_b1), chunks(L0_ffn_fc1_bias),
                             column(np.repeat(np.asarray(L0_attn_gamma), AD))], axis=1)
    rows = np.concatenate([np.asarray(v).reshape(-1) for v in (
        L0_xattn_bo, L0_xattn_b2, L0_attn_bo, L0_ffn_fc2_bias, L0_attn_bv, L0_ffn_fc1_scales,
        L0_ffn_fc2_scales)])
    p = np.arange(P)
    consts = np.zeros((P, CCW), np.float32)
    consts[:, C_ID:C_ID + P] = np.eye(P)
    consts[:, C_CAUSAL:C_CAUSAL + TOK] = (p[:, None] % TOK) <= np.arange(TOK)[None, :]
    consts[:, C_HEAD:C_HEAD + ROWG] = (p[:, None] % (ROWG * AD)) // AD == np.arange(ROWG)[None, :]
    consts[:, C_GRP:C_GRP + ROWG] = p[:, None] // (ROWG * AD) == np.array([0, 2, 1, 3])[None, :]
    consts[:, C_H8:C_H8 + 8] = (p[:, None] % (8 * AD)) // AD == np.arange(8)[None, :]
    consts[:, C_IDX:C_IDX + TOK] = np.arange(TOK)[None, :]
    chunk_select = np.repeat(np.eye(2 * MC, dtype=np.float32), TOK, axis=1)

    arrays = {
        "x": lay(x[0]), "ctx": lay(ctx_1024[0]), "wq": lay(L0_xattn_wq), "wk": lay(L0_xattn_wk), "wv": lay(L0_xattn_wv),
        "wo": lay(L0_xattn_wo), "w1": lay(L0_xattn_w1), "w2": lay(L0_xattn_w2), "wqT": lay(np.asarray(L0_attn_Wq).T),
        "wkT": lay(np.asarray(L0_attn_Wk).T), "wvT": lay(np.asarray(L0_attn_Wv).T), "woT": lay(np.asarray(L0_attn_Wo).T),
        "fc1": lay(L0_ffn_fc1_q), "fc2": lay(L0_ffn_fc2_q), "cols_consts": lay(np.concatenate([consts, cols], axis=1)), "rows": lay(rows),
        "chunk_select": chunk_select,
    }
    nc = bacc.Bacc("TRN2", target_bir_lowering=False, num_devices=1)
    feeds, args = {}, []
    for name, a in arrays.items():
        feeds[f"in_{name}"] = a
        args.append(nc.dram_tensor(f"in_{name}", a.shape, mb.dt.from_np(a.dtype), kind="ExternalInput").ap())
    result = nc.dram_tensor("result", (1, TOK, D), mb.dt.float32, kind="ExternalOutput").ap()
    build_kernel(nc, *args, result[0])
    r = run_bass_kernel_spmd(nc, [feeds], core_ids=[0])
    return r.results[0]["result"]
```

```python
from contextlib import ExitStack

import concourse.bass as bass
from concourse import mybir

F32 = mybir.dt.float32
F32R = mybir.dt.float32r
I32 = mybir.dt.int32
ALU = mybir.AluOpType
ACT = mybir.ActivationFunctionType
AX_X = mybir.AxisListType.X

P = 128
D = 128
TOK = 64
CTX = 6272
TILES = CTX // P
GROUP = 4
BODY = 8
ITERS = (TILES - 1) // BODY
XH, XD = 16, 64
INNER = XH * XD
PAIRS = INNER // P
HALF = INNER // 2
HH = XH // 2
MLP = 512
MC = MLP // P
AH, AD = 16, 8
ROWG = 4
EPS = 1e-5
TINY = 1e-12
KN = 4
WARM = 7

CW = 9 + 2 * MC
C_B1 = 8
C_GAM = 8 + 2 * MC
R_BO, R_B2, R_ABO, R_FB2, R_BV, R_S1, R_S2 = 0, 128, 256, 384, 512, 640, 1152
RW = 1664
C_ID, C_CAUSAL, C_HEAD, C_GRP, C_H8 = 0, 128, 192, 196, 200
CCW = 208
FIRST_SPLIT = 1 + GROUP


def build_kernel(nc, x, ctx_rows, wq, wk, wv, wo, w1, w2, wqT, wkT, wvT, woT, fc1, fc2, cols_consts, rows,
                 chunk_select, out):
    ctx = ExitStack()
    with ctx:
        def sb(name, shape, dt=F32):
            return ctx.enter_context(nc.sbuf_tensor(name, shape, dt))

        def sem(name):
            return ctx.enter_context(nc.semaphore(name))

        cst_col = sb("cst_col", [P, CCW + CW])
        cst = cst_col[:, 0:CCW]
        col = cst_col[:, CCW:CCW + CW]
        row = sb("row", [P, RW])
        sel = sb("sel", [2 * MC, 2 * MC * TOK])
        xs = sb("xs", [TOK, D])
        wq_s = sb("wq_s", [P, INNER])
        wk_s = sb("wk_s", [P, INNER])
        wv_s = sb("wv_s", [P, INNER])
        wo_s = sb("wo_s", [P, PAIRS, D])
        w1_s = sb("w1_s", [P, MLP])
        w2_s = sb("w2_s", [P, MC, D])
        attn_w = sb("attn_w", [P, 4, D])
        fc1_q = sb("fc1_q", [P, MLP], I32)
        fc2_q = sb("fc2_q", [P, MC, D], I32)
        ident = cst[:, C_ID:C_ID + P]
        ctx_s = sb("ctx_s", [P, 3, GROUP, D])
        z = sb("z", [P, 3, GROUP, D])
        z_hi = sb("z_hi", [P, 2, GROUP, D], F32R)
        one_zero = sb("one_zero", [P, 2])
        z_lo = sb("z_lo", [P, 2, GROUP, D], F32R)
        ident_r = sb("ident_r", [P, P], F32R)
        zT_hi = sb("zT_hi", [P, 3, GROUP * P], F32R)
        zT_lo = sb("zT_lo", [P, 3, GROUP * P], F32R)
        bn = sb("bn", [P, 3, GROUP, 6])
        mv = sb("mv", [P, 3, GROUP, 2])
        ln_std = sb("ln_std", [P, 3, GROUP])
        ln_r = sb("ln_r", [P, 3, GROUP])
        ln_mr = sb("ln_mr", [P, 3, GROUP])
        ln_c = sb("ln_c", [P, 3, GROUP])
        k_sq = sb("k_sq", [P, 2, INNER])
        n2 = sb("n2", [P, KN, XH])
        nrm = sb("nrm", [P, KN, XH])
        rinv = sb("rinv", [P, KN, XH])
        kn = sb("kn", [P, KN, INNER])
        kn_hi = sb("kn_hi", [P, KN, HALF], F32R)
        kn_lo = sb("kn_lo", [P, KN, HALF], F32R)
        fold_d = sb("fold_d", [P, 2])
        fold = sb("fold", [P, P])
        wk_hi = sb("wk_hi", [P, INNER], F32R)
        wk_lo = sb("wk_lo", [P, INNER], F32R)
        wv_f = sb("wv_f", [P, INNER])
        x_bn = sb("x_bn", [TOK, 6])
        x_mv = sb("x_mv", [TOK, 2])
        x_std = sb("x_std", [TOK, 2])
        x_r = sb("x_r", [TOK, 2])
        xl = sb("xl", [TOK, D])
        xl_bo = sb("xl_bo", [TOK, D])
        x_b2 = sb("x_b2", [TOK, D])
        xq = sb("xq", [TOK, D])
        xqT = sb("xqT", [P, TOK])
        q_sq = sb("q_sq", [TOK, INNER])
        q_n2 = sb("q_n2", [TOK, 2, XH // 2])
        q_nrm = sb("q_nrm", [TOK, 2, XH // 2])
        q_rinv = sb("q_rinv", [TOK, 2, XH // 2])
        qn = sb("qn", [TOK, INNER])
        qnT = sb("qnT", [P, PAIRS, TOK])
        w1_g = sb("w1_g", [P, MLP])
        fc1_d = sb("fc1_d", [P, MLP])
        fc1_f = sb("fc1_f", [P, MLP])
        fc1_g = sb("fc1_g", [P, MLP])
        fc2_f = sb("fc2_f", [P, MC, D])
        fc2_d = sb("fc2_d", [P, MC, D])
        bias_c = sb("bias_c", [P, 2 * MC])
        biasT = sb("biasT", [2 * MC, P])
        decay = sb("decay", [P, TOK])
        gam_pow = sb("gam_pow", [P, 7])
        decay_heads = sb("decay_heads", [P, 8, TOK])
        half_neg = sb("half_neg", [TOK, 2])
        warm = sb("warm", [TOK, 2])
        eps_tile = sb("eps_tile", [P, 2])
        zeros = sb("zeros", [P, HALF], mybir.dt.bfloat16)
        ones_row = sb("ones_row", [1, P])
        gT = sb("gT", [P, INNER])
        m_bd = sb("m_bd", [P, PAIRS, P])
        oT = sb("oT", [P, PAIRS, TOK])
        x1 = sb("x1", [TOK, D])
        x1_r = sb("x1_r", [TOK, D])
        t_bn = sb("t_bn", [TOK, 3, 6])
        t_mv = sb("t_mv", [TOK, 3, 2])
        t_ve = sb("t_ve", [TOK, 3, 2])
        t_r = sb("t_r", [TOK, 3, 2])
        t_hat = sb("t_hat", [TOK, 3, D])
        hatT = sb("hatT", [P, 3, P])
        h1 = sb("h1", [P, MC * TOK])
        x2 = sb("x2", [TOK, D])
        x2_r = sb("x2_r", [TOK, D])
        q_heads = sb("q_heads", [P, ROWG, TOK])
        k_groups = sb("k_groups", [P, ROWG, TOK])
        v_bd = sb("v_bd", [P, D])
        scores = sb("scores", [P, 8, TOK])
        a_heads = sb("a_heads", [P, 8, TOK])
        a_outT = sb("a_outT", [P, TOK])
        x3 = sb("x3", [TOK, D])
        u = sb("u", [TOK, D])
        x3_u = sb("x3_u", [TOK, D])
        fb_half = sb("fb_half", [TOK, D])
        x3_r = sb("x3_r", [TOK, D])
        h2 = sb("h2", [P, MC * TOK])
        y_out = sb("y_out", [TOK, D])
        ps = ctx.enter_context(nc.psum_tensor("ps", [P, 8, 512], F32))
        g_ps = ps[:, 0:2, :]
        k_ps = [ps[:, 2:4, :], ps[:, 4:6, :]]
        zT_hi_ps = ps[:, 6, :].bitcast(F32R)
        zT_lo_ps = ps[:, 7, :].bitcast(F32R)
        misc = ps[:, 7, :]

        in_small = sem("in_small")
        in_x = sem("in_x")
        in_wk = [sem("in_wk0"), sem("in_wk1")]
        in_wq = sem("in_wq")
        in_wv = sem("in_wv")
        in_row = sem("in_row")
        in_pool_w = sem("in_pool_w")
        in_tail_w = sem("in_tail_w")
        ctx_in = [sem("ctx_in0"), sem("ctx_in1"), sem("ctx_in_lead")]
        var_ready = sem("var_ready")
        std_ready = sem("std_ready")
        bn_ready = sem("bn_ready")
        r_ready = sem("r_ready")
        mr_ready = sem("mr_ready")
        zc_ready = sem("zc_ready")
        z_ready = sem("z_ready")
        z_hi_ready = sem("z_hi_ready")
        z_hi2_ready = sem("z_hi2_ready")
        z_lo_ready = sem("z_lo_ready")
        ident_ready = sem("ident_ready")
        zT_ready = sem("zT_ready")
        hi_ready = sem("hi_ready")
        lo_ready = sem("lo_ready")
        k_ready = sem("k_ready")
        sq_ready = sem("sq_ready")
        n2_ready = sem("n2_ready")
        nrm_ready = sem("nrm_ready")
        rinv_ready = sem("rinv_ready")
        kn_ready = sem("kn_ready")
        kn_hi_ready = sem("kn_hi_ready")
        kn_lo_ready = sem("kn_lo_ready")
        g_added = sem("g_added")
        fold_ready = sem("fold_ready")
        wkf_ready = sem("wkf_ready")
        wk_hi_ready = sem("wk_hi_ready")
        wk_lo_ready = sem("wk_lo_ready")
        wvf_ready = sem("wvf_ready")
        wv_ready = sem("wv_ready")
        x_stat = sem("x_stat")
        x_std_ready = sem("x_std_ready")
        xq_ready = sem("xq_ready")
        xqT_ps = sem("xqT_ps")
        xqT_ready = sem("xqT_ready")
        q_ready = sem("q_ready")
        q_sq_ready = sem("q_sq_ready")
        q_n2_ready = sem("q_n2_ready")
        q_nrm_ready = sem("q_nrm_ready")
        q_step = sem("q_step")
        qn_ready = sem("qn_ready")
        qnT_ps = sem("qnT_ps")
        qnT_ready = sem("qnT_ready")
        xl_ready = sem("xl_ready")
        res_ready = sem("res_ready")
        pool_step = sem("pool_step")
        w1g_ready = sem("w1g_ready")
        fc1_ready = sem("fc1_ready")
        fc2_ready = sem("fc2_ready")
        decay_step = sem("decay_step")
        decay_ready = sem("decay_ready")
        zero_ready = sem("zero_ready")
        one_zero_ready = sem("one_zero_ready")
        eps_ready = sem("eps_ready")
        warm_done = sem("warm_done")
        bias_ps = sem("bias_ps")
        bias_col = sem("bias_col")
        biasT_ps = sem("biasT_ps")
        biasT_ready = sem("biasT_ready")
        gT_ready = sem("gT_ready")
        m_ready = sem("m_ready")
        gT_hi_ready = sem("gT_hi_ready")
        mbd_lo_ready = sem("mbd_lo_ready")
        mbd_hi_ready = sem("mbd_hi_ready")
        oT_hi_ready = sem("oT_hi_ready")
        oT_ps = sem("oT_ps")
        oT_ready = sem("oT_ready")
        y1_ready = sem("y1_ready")
        x_ready = sem("x_ready")
        tbn_ready = sem("tbn_ready")
        tmv_ready = sem("tmv_ready")
        ve_ready = sem("ve_ready")
        tr_ready = sem("tr_ready")
        hat_ready = sem("hat_ready")
        hatT_ps = sem("hatT_ps")
        hatT_ready = sem("hatT_ready")
        h1_ps = sem("h1_ps")
        h1_ready = sem("h1_ready")
        y2_ready = sem("y2_ready")
        rest_ready = sem("rest_ready")
        u_ready = sem("u_ready")
        qkv_ps = sem("qkv_ps")
        qk_ready = sem("qk_ready")
        v_ready = sem("v_ready")
        s_ps = sem("s_ps")
        s_ready = sem("s_ready")
        ao_ps = sem("ao_ps")
        ao_ready = sem("ao_ready")
        aoT_ready = sem("aoT_ready")
        y3_ready = sem("y3_ready")
        h2_ps = sem("h2_ps")
        h2_ready = sem("h2_ready")
        y4_ready = sem("y4_ready")
        final_ready = sem("final_ready")
        stored = sem("stored")

        ctx_v = ctx_rows.rearrange("(p t) d -> p t d", t=TILES)
        heads = lambda ap: ap.rearrange("p (h d) -> p h d", h=XH)

        def where(s_in_body):
            return (s_in_body // GROUP) % 2, s_in_body % GROUP

        block = ctx.enter_context(nc.Block())

        @block.sync
        def _(sp):
            sp.dma_start(cst_col[:, :], cols_consts).then_inc(in_small, 16)
            sp.dma_start(ctx_s[:, 2, 0:1, :], ctx_v[:, 0:1, :]).then_inc(ctx_in[2], 16)
            for g in range(2):
                sp.dma_start(ctx_s[:, g, :, :], ctx_v[:, 1 + GROUP * g:1 + GROUP * (g + 1), :]).then_inc(ctx_in[g], 16)
            sp.dma_start(w1_s[:, :], w1).then_inc(in_pool_w, 16)
            sp.dma_start(fc1_q[:, :], fc1).then_inc(in_pool_w, 16)
            sp.dma_start(fc2_q[:, :, :], fc2.rearrange("(c p) n -> p c n", c=MC)).then_inc(in_pool_w, 16)

            def next_group(i, g):
                sp.wait_ge(z_ready, i * BODY + 1 + GROUP * (g + 1))
                first = i * BODY + 1 + GROUP * (2 + g)
                sp.dma_start(ctx_s[:, g, :, :], ctx_v[:, bass.ds(first, GROUP), :]).then_inc(ctx_in[g], 16)

            next_group(0, 0)
            sp.dma_start(sel[:, :], chunk_select).then_inc(in_tail_w, 16)
            sp.dma_start(wv_s[:, :], wv).then_inc(in_wv, 16)
            sp.dma_start(wo_s[:, :, :], wo.rearrange("(c p) n -> p c n", c=PAIRS)).then_inc(in_tail_w, 16)
            sp.dma_start(w2_s[:, :, :], w2.rearrange("(c p) n -> p c n", c=MC)).then_inc(in_tail_w, 16)
            for n, w in enumerate((wqT, wkT, wvT, woT)):
                sp.dma_start(attn_w[:, n, :], w).then_inc(in_tail_w, 16)
            next_group(0, 1)
            with sp.Fori(1, ITERS - 1) as i:
                for g in range(2):
                    next_group(i, g)
            sp.wait_ge(final_ready, 1)
            sp.dma_start(out, y_out[:, :]).then_inc(stored, 16)
            sp.wait_ge(stored, 16)

        @block.gpsimd
        def _(pool):
            nc.gpsimd.memset(half_neg[:, :], -0.5).then_inc(pool_step, 1)
            nc.gpsimd.memset(one_zero[:, 0:1], 1.0).then_inc(one_zero_ready, 1)
            nc.gpsimd.memset(one_zero[:, 1:2], 0.0).then_inc(one_zero_ready, 1)
            nc.gpsimd.memset(m_bd[:, :, :], 0.0).then_inc(zero_ready, 1)
            nc.gpsimd.memset(ones_row[:, :], 1.0).then_inc(zero_ready, 1)
            nc.gpsimd.memset(v_bd[:, :], 0.0).then_inc(zero_ready, 1)
            pool.wait_ge(in_wk[1], 16)
            pool.dma_start(row[:, :], rows.partition_broadcast(P)).then_inc(in_row, 16)
            pool.wait_ge(one_zero_ready, 2)

            def z_shift(slot, group):
                pool.wait_ge(r_ready, group + 2)
                nc.gpsimd.tensor_tensor(ln_mr[:, slot, :], mv[:, slot, :, 0], ln_r[:, slot, :],
                                        ALU.mult).then_inc(mr_ready, 1)
                pool.wait_ge(mr_ready, group + 2)
                nc.gpsimd.tensor_tensor(ln_c[:, slot, :], one_zero[:, 0:1].broadcast_to([P, GROUP]), ln_mr[:, slot, :],
                                        ALU.subtract).then_inc(zc_ready, 1)

            def z_high(slot, group):
                pool.wait_ge(z_ready, group * GROUP + 3)
                nc.gpsimd.tensor_tensor(z_hi[:, slot, 0:2, :], z[:, slot, 0:2, :],
                                        one_zero[:, 1:2].unsqueeze(2).broadcast_to([P, 2, D]),
                                        ALU.add).then_inc(z_hi_ready, 1)

            def z_low(slot, places, high_ready, group):
                a, b = places
                pool.wait_ge(high_ready, group)
                nc.gpsimd.tensor_tensor(z_lo[:, slot, a:b, :], z[:, slot, a:b, :], z_hi[:, slot, a:b, :].bitcast(F32),
                                        ALU.subtract).then_inc(z_lo_ready, 1)

            def kn_low(s, buf):
                pool.wait_ge(kn_hi_ready, s - (FIRST_SPLIT - 1))
                nc.gpsimd.tensor_tensor(kn_lo[:, buf, :], kn[:, buf, HALF:INNER], kn_hi[:, buf, :].bitcast(F32),
                                        ALU.subtract).then_inc(kn_lo_ready, 1)

            def weight_extra(j):
                if j == 0:
                    pool.wait_ge(in_small, 16)
                    pool.wait_ge(in_pool_w, 48)
                    pool.wait_ge(in_row, 16)
                    nc.gpsimd.tensor_scalar(w1_g[:, :], w1_s[:, :], col[:, 2:3], 0.0, ALU.mult,
                                            ALU.add).then_inc(w1g_ready, 1)
                    nc.gpsimd.tensor_scalar(fc1_f[:, :], fc1_q[:, :], -128.0, 1.0, ALU.add, ALU.mult).then_inc(pool_step, 1)
                elif j == 1:
                    nc.gpsimd.tensor_scalar(fc2_f[:, :, :], fc2_q[:, :, :], -128.0, 1.0, ALU.add,
                                            ALU.mult).then_inc(pool_step, 1)
                elif j == 2:
                    pool.wait_ge(pool_step, 2)
                    nc.gpsimd.tensor_tensor(fc1_d[:, :], fc1_f[:, :], row[:, R_S1:R_S1 + MLP], ALU.mult).then_inc(pool_step, 1)
                elif j == 3:
                    pool.wait_ge(pool_step, 3)
                    nc.gpsimd.tensor_tensor(fc2_d[:, :, :], fc2_f[:, :, :],
                                            row[:, R_S2:R_S2 + MLP].rearrange("p (c n) -> p c n", c=MC),
                                            ALU.mult).then_inc(fc2_ready, 1)
                elif j == 4:
                    pool.wait_ge(pool_step, 4)
                    nc.gpsimd.tensor_scalar(fc1_g[:, :], fc1_d[:, :], col[:, 4:5], 0.0, ALU.mult,
                                            ALU.add).then_inc(fc1_ready, 1)
                    nc.gpsimd.memset(decay[:, 0:1], 1.0).then_inc(decay_step, 1)
                    nc.gpsimd.tensor_scalar(gam_pow[:, 0:1], col[:, C_GAM:C_GAM + 1], 1.0, 0.0, ALU.mult,
                                            ALU.add).then_inc(decay_step, 1)
                elif j in (5, 6):
                    for m in range(3 * (j - 5), 3 * (j - 4)):
                        n = 1 << m
                        pool.wait_ge(decay_step, 2 * m + 2)
                        nc.gpsimd.tensor_scalar(decay[:, n:2 * n], decay[:, 0:n], gam_pow[:, m:m + 1], 0.0, ALU.mult,
                                                ALU.add).then_inc(decay_step, 1)
                        nc.gpsimd.tensor_tensor(gam_pow[:, m + 1:m + 2], gam_pow[:, m:m + 1], gam_pow[:, m:m + 1],
                                                ALU.mult).then_inc(decay_step, 1)
                else:
                    pool.wait_ge(decay_step, 14)
                    nc.gpsimd.tensor_tensor(decay_heads[:, :, :], decay[:, :].unsqueeze(1).broadcast_to([P, 8, TOK]),
                                            cst[:, C_H8:C_H8 + 8].unsqueeze(2).broadcast_to([P, 8, TOK]),
                                            ALU.mult).then_inc(decay_ready, 1)

            def residual_extra(j):
                if j == 0:
                    pool.wait_ge(x_stat, 3)
                    nc.gpsimd.tensor_scalar(xl[:, :], xs[:, :], x_mv[:, 0:1], x_r[:, 0:1],
                                            ALU.subtract, ALU.mult).then_inc(xl_ready, 1)
                    nc.gpsimd.tensor_scalar(fb_half[:, :], row[0:TOK, R_FB2:R_FB2 + D], 0.5, 0.0,
                                            ALU.mult, ALU.add).then_inc(res_ready, 1)
                elif j == 4:
                    pool.wait_ge(xl_ready, 1)
                    nc.gpsimd.tensor_tensor(xl_bo[:, :], xl[:, :], row[0:TOK, R_BO:R_BO + D], ALU.add).then_inc(res_ready, 1)
                    nc.gpsimd.tensor_tensor(x_b2[:, :], xs[:, :], row[0:TOK, R_B2:R_B2 + D], ALU.add).then_inc(res_ready, 1)

            def body(i, first=False, last=False):
                for j in range(BODY):
                    s = i * BODY + (1 + j)
                    slot, place = where(j + GROUP)
                    group = i * 2 + (j // GROUP + 1)
                    prepare = not (last and j >= GROUP)
                    if place == 0 and prepare:
                        z_shift(slot, group)
                    if not first or j > GROUP:
                        kn_low(s - 1, j % KN)
                    if place == 0 and prepare:
                        z_high(slot, group)
                        z_low(slot, (0, 2), z_hi_ready, group)
                    if place == 1 and prepare:
                        z_low(slot, (2, GROUP), z_hi2_ready, group)
                    if first:
                        weight_extra(j)
                    if last:
                        residual_extra(j)

            body(0, first=True)
            with pool.Fori(1, ITERS - 1) as i:
                body(i)
            body(ITERS - 1, last=True)
            for n, which in ((0, 0), (1, 0), (2, 1), (2, 0)):
                pool.wait_ge(ve_ready, n + which + 1 if n < 2 else 4 - which)
                nc.gpsimd.tensor_tensor(t_r[:, n, which:which + 1], t_ve[:, n, which:which + 1], half_neg[:, 0:1],
                                        ALU.pow).then_inc(tr_ready, 1)

        @block.scalar
        def _(act):
            for half in range(2):
                c = slice(half * HALF, (half + 1) * HALF)
                act.dma_start(wk_s[:, c], wk[:, c]).then_inc(in_wk[half], 16)
            act.wait_ge(eps_ready, 2)
            nc.scalar.activation(warm[:, 0:1], eps_tile[0:TOK, 0:1], ACT.Sqrt).then_inc(warm_done, 1)
            act.dma_start(xs[:, :], x).then_inc(in_x, 16)
            act.dma_start(wq_s[:, :], wq).then_inc(in_wq, 16)

            def group_std(slot, count, group):
                act.wait_ge(var_ready, group + 2 if type(group) is int and group < 2 else group * 3)
                nc.scalar.activation(ln_std[:, slot, 0:count], mv[:, slot, 0:count, 1], ACT.Sqrt, bias=eps_c(0),
                                     scale=1.0).then_inc(std_ready, 1)

            def zT_high(slot, set_no, first=0, end=GROUP, bank=6):
                act.wait_ge(zT_ready, set_no)
                nc.scalar.activation(zT_hi[:, slot, first * P:end * P], ps[:, bank, first * P:end * P],
                                     ACT.Copy).then_inc(hi_ready, 1)

            def zT_out(slot, set_no):
                act.wait_ge(zT_ready, set_no)
                nc.scalar.activation(zT_hi[:, slot, :], zT_hi_ps.bitcast(F32), ACT.Copy).then_inc(hi_ready, 1)
                nc.scalar.activation(zT_lo[:, slot, :], zT_lo_ps.bitcast(F32), ACT.Copy).then_inc(lo_ready, 1)

            def kn_high(s, buf):
                act.wait_ge(kn_ready, s * 2 + 2)
                nc.scalar.activation(kn_hi[:, buf, :], kn[:, buf, HALF:INNER], ACT.Copy).then_inc(kn_hi_ready, 1)

            def make_z(slot, places, group):
                act.wait_ge(zc_ready, group + 2)
                for j in places:
                    if not (type(group) is int and group < 2):
                        act.wait_ge(g_added, group * GROUP + (j + 2 - 2 * GROUP))
                    nc.scalar.activation(z[:, slot, j, :], ctx_s[:, slot, j, :], ACT.Identity,
                                         bias=ln_c[:, slot, j:j + 1], scale=ln_r[:, slot, j:j + 1]).then_inc(z_ready, 1)

            def square(s, buf):
                for half in range(2):
                    act.wait_ge(k_ready, s * 2 + (1 + half))
                    if not (type(s) is int and s < 2):
                        act.wait_ge(n2_ready, s * 2 + (half - 3))
                    nc.scalar.activation(k_sq[:, buf, half * HALF:(half + 1) * HALF], k_ps[buf][:, half, :],
                                         ACT.Square).then_inc(sq_ready, 1)

            def norm(s, buf, half):
                act.wait_ge(n2_ready, s * 2 + (1 + half))
                nc.scalar.activation(nrm[:, buf, half * HH:(half + 1) * HH], n2[:, buf, half * HH:(half + 1) * HH],
                                     ACT.Sqrt).then_inc(nrm_ready, 1)

            def eps_c(n, p=P):
                return eps_tile[0:p, n:n + 1]

            def query_part(half, j):
                c = slice(half * HALF, (half + 1) * HALF)
                if j == 0 and half == 0:
                    act.wait_ge(x_stat, 2)
                    nc.scalar.activation(x_std[:, 0:1], x_mv[:, 1:2], ACT.Sqrt, bias=eps_c(0, TOK),
                                         scale=1.0).then_inc(x_std_ready, 1)
                    nc.scalar.activation(x_std[:, 1:2], x_mv[:, 1:2], ACT.Sqrt, bias=eps_c(1, TOK),
                                         scale=1.0 + EPS).then_inc(x_std_ready, 1)
                elif j == 1 and half == 0:
                    act.wait_ge(xqT_ps, 1)
                    nc.scalar.activation(xqT[:, :], misc[:, 0:TOK], ACT.Identity, bias=col[:, 1:2],
                                         scale=col[:, 0:1]).then_inc(xqT_ready, 1)
                elif j == 3:
                    act.wait_ge(q_ready, half + 1)
                    nc.scalar.activation(q_sq[:, c], misc[0:TOK, :], ACT.Square).then_inc(q_sq_ready, 1)
                elif j == 4:
                    act.wait_ge(q_n2_ready, half + 1)
                    nc.scalar.activation(q_nrm[:, half, :], q_n2[:, half, :], ACT.Sqrt).then_inc(q_nrm_ready, 1)

            def weight_extra(j):
                if j in (0, 1):
                    act.wait_ge(wvf_ready, j + 1)
                    nc.scalar.activation(wv_f[:, j * HALF:(j + 1) * HALF], misc, ACT.Copy).then_inc(wv_ready, 1)
                elif j == 5:
                    act.wait_ge(qnT_ps, 1)
                    nc.scalar.activation(qnT[:, :, :], misc.rearrange("p (c t) -> p c t", t=TOK),
                                         ACT.Copy).then_inc(qnT_ready, 1)

            group_std(2, 1, -1)
            make_z(2, range(1), -1)
            for half in range(2):
                act.wait_ge(wkf_ready, half + 1)
                nc.scalar.activation(wk_hi[:, half * HALF:(half + 1) * HALF], k_ps[0][:, half, :],
                                     ACT.Copy).then_inc(wk_hi_ready, 1)
                if half == 0:
                    group_std(0, GROUP, 0)
                    zT_high(2, 1, end=1)
            make_z(0, range(1), 0)
            zT_high(0, 2, end=1, bank=7)
            make_z(0, range(1, 3), 0)
            square(0, 0)
            make_z(0, range(3, GROUP), 0)
            norm(0, 0, 0)
            norm(0, 0, 1)
            zT_high(0, 3, first=1)

            def body(i, first=False, last=False):
                for j in range(BODY):
                    s = i * BODY + (1 + j)
                    slot, place = where(j + GROUP)
                    group = i * 2 + (j // GROUP + 1)
                    prepare = not (last and j >= GROUP)
                    if place == 0 and prepare:
                        group_std(slot, GROUP, group)
                    square(s, (1 + j) % 2)
                    if not first or j > GROUP:
                        kn_high(s - 1, j % KN)
                    norm(s, (1 + j) % KN, 0)
                    if place in (0, 1) and prepare:
                        make_z(slot, range(2 * place, 2 * place + 1), group)
                    norm(s, (1 + j) % KN, 1)
                    if place in (0, 1) and prepare:
                        make_z(slot, range(2 * place + 1, 2 * place + 2), group)
                    if place == 1 and prepare:
                        act.wait_ge(z_ready, group * GROUP + (GROUP + 1))
                        nc.scalar.activation(z_hi[:, slot, 2:GROUP, :], z[:, slot, 2:GROUP, :],
                                             ACT.Copy).then_inc(z_hi2_ready, 1)
                    if first:
                        query_part(0, j)
                    if place == 2 and prepare:
                        zT_out(slot, group + 3)
                    if last:
                        query_part(1, j)
                        weight_extra(j)

            body(0, first=True)
            with act.Fori(1, ITERS - 1) as i:
                body(i)
            body(ITERS - 1, last=True)
            act.wait_ge(pool_step, 1)
            act.wait_ge(warm_done, 1)
            nc.scalar.activation(warm[:, 0:1], half_neg[:, 0:1], ACT.Gelu).then_inc(warm_done, 1)
            act.wait_ge(g_added, TILES)
            nc.scalar.activation(gT[:, 0:HALF], ps[:, 0, :], ACT.Copy).then_inc(gT_ready, 1)
            act.wait_ge(zero_ready, 1)
            for half in range(2):
                act.wait_ge(m_ready, half + 1)
                nc.scalar.activation(m_bd[0:XD, 4 * half:4 * half + 4, 0:XD],
                                     ps[0:XD, 2 + half, :].rearrange("p (c n) -> p c n", n=P)[:, :, 0:XD],
                                     ACT.Copy).then_inc(mbd_lo_ready, 1)
            act.wait_ge(oT_ps, 1)
            nc.scalar.activation(oT[:, 0:PAIRS // 2, :], ps[:, 4, 0:256], ACT.Copy).then_inc(oT_ready, 1)
            act.wait_ge(h1_ps, 1)
            nc.scalar.activation(h1[:, :], ps[:, 7, 0:MC * TOK], ACT.Gelu).then_inc(h1_ready, 1)
            act.wait_ge(warm_done, 2)
            nc.scalar.activation(warm[:, 1:2], half_neg[:, 0:1], ACT.Silu).then_inc(warm_done, 1)
            act.wait_ge(qkv_ps, 3)
            act.wait_ge(zero_ready, 3)
            for half in range(2):
                at = 64 * half
                nc.scalar.activation(v_bd[at:at + 64, at:at + 64], ps[at:at + 64, 1, 256 + at:320 + at],
                                     ACT.Copy).then_inc(v_ready, 1)
            act.wait_ge(h2_ps, 1)
            nc.scalar.activation(h2[:, :], ps[:, 7, 0:MC * TOK], ACT.Silu).then_inc(h2_ready, 1)

        @block.vector
        def _(dve):
            def stats(slot, places):
                for j in places:
                    nc.vector.bn_stats(bn[:, slot, j, :], ctx_s[:, slot, j, :]).then_inc(bn_ready, 1)

            def aggregate(slot, places):
                for j in places:
                    last = nc.vector.bn_aggr(mv[:, slot, j, :], bn[:, slot, j, :])
                last.then_inc(var_ready, 1)

            def rstd(slot, count, group):
                dve.wait_ge(std_ready, group + 2)
                nc.vector.reciprocal(ln_r[:, slot, 0:count], ln_std[:, slot, 0:count]).then_inc(r_ready, 1)

            def z_scalars(slot, count, group):
                rstd(slot, count, group)
                dve.wait_ge(r_ready, group + 2)
                nc.vector.tensor_tensor(ln_mr[:, slot, 0:count], mv[:, slot, 0:count, 0], ln_r[:, slot, 0:count],
                                        ALU.mult).then_inc(mr_ready, 1)
                dve.wait_ge(mr_ready, group + 2)
                nc.vector.tensor_scalar(ln_c[:, slot, 0:count], ln_mr[:, slot, 0:count], -1.0, 1.0,
                                        ALU.mult, ALU.add).then_inc(zc_ready, 1)

            def zT_low(slot, set_no, first=0, end=GROUP, bank=6):
                dve.wait_ge(hi_ready, set_no)
                nc.vector.tensor_tensor(zT_lo[:, slot, first * P:end * P], ps[:, bank, first * P:end * P],
                                        zT_hi[:, slot, first * P:end * P].bitcast(F32),
                                        ALU.subtract).then_inc(lo_ready, 1)

            def head_sums(s, sq, buf, half):
                dve.wait_ge(sq_ready, s * 2 + (1 + half))
                nc.vector.tensor_reduce(n2[:, buf, half * HH:(half + 1) * HH],
                                        heads(k_sq[:, sq, :])[:, half * HH:(half + 1) * HH, :], AX_X,
                                        ALU.add).then_inc(n2_ready, 1)

            def inverse(s, buf, half):
                h = slice(half * HH, (half + 1) * HH)
                dve.wait_ge(nrm_ready, s * 2 + (1 + half))
                nc.vector.reciprocal(rinv[:, buf, h], nrm[:, buf, h]).then_inc(rinv_ready, 1)

            def normalise(s, kbuf, buf, half):
                h = slice(half * HH, (half + 1) * HH)
                dve.wait_ge(rinv_ready, s * 2 + (1 + half))
                if half == 0 and not (type(s) is int and s < KN):
                    dve.wait_ge(g_added, s - KN + 1)
                nc.vector.scalar_tensor_tensor(
                    heads(kn[:, buf, :])[:, h, :], rinv[:, buf, h].unsqueeze(2).broadcast_to([P, HH, XD]), 1.0 / TINY,
                    k_ps[kbuf][:, half, :].rearrange("p (h d) -> p h d", d=XD),
                    ALU.min, ALU.mult).then_inc(kn_ready, 1)

            nc.vector.memset(eps_tile[:, 0:1], EPS).then_inc(eps_ready, 1)
            nc.vector.memset(eps_tile[:, 1:2], EPS * EPS).then_inc(eps_ready, 1)
            nc.vector.memset(zeros[:, :], 0.0).then_inc(eps_ready, 1)
            dve.wait_ge(in_small, 16)
            nc.vector.tensor_tensor(fold_d[:, 0:1], col[:, 1:2], col[:, 0:1], ALU.subtract).then_inc(fold_ready, 1)
            dve.wait_ge(fold_ready, 1)
            nc.vector.tensor_scalar(fold_d[:, 1:2], fold_d[:, 0:1], 1.0 / D, None, ALU.mult).then_inc(fold_ready, 1)
            dve.wait_ge(fold_ready, 2)
            nc.vector.tensor_scalar(fold[:, :], ident, col[:, 0:1], fold_d[:, 1:2], ALU.mult, ALU.add).then_inc(fold_ready, 1)
            nc.vector.tensor_copy(ident_r[:, :], ident).then_inc(ident_ready, 1)
            dve.wait_ge(ctx_in[2], 16)
            stats(2, range(1))
            dve.wait_ge(bn_ready, 1)
            aggregate(2, range(1))
            z_scalars(2, 1, -1)
            dve.wait_ge(ctx_in[0], 16)
            stats(0, range(GROUP))
            dve.wait_ge(bn_ready, 1 + GROUP)
            aggregate(0, range(GROUP))
            for half in range(2):
                dve.wait_ge(wk_hi_ready, half + 1)
                nc.vector.tensor_tensor(wk_lo[:, half * HALF:(half + 1) * HALF], k_ps[0][:, half, :],
                                        wk_hi[:, half * HALF:(half + 1) * HALF].bitcast(F32),
                                        ALU.subtract).then_inc(wk_lo_ready, 1)
                if half == 0:
                    z_scalars(0, GROUP, 0)
                    dve.wait_ge(in_x, 16)
                    nc.vector.bn_stats(x_bn[:, :], xs[:, :]).then_inc(x_stat, 1)
                    zT_low(2, 1, end=1)
            dve.wait_ge(x_stat, 1)
            nc.vector.bn_aggr(x_mv[:, :], x_bn[:, :]).then_inc(x_stat, 1)
            zT_low(0, 2, end=1, bank=7)
            dve.wait_ge(ctx_in[1], 16)
            stats(1, range(GROUP))
            head_sums(0, 0, 0, 0)
            head_sums(0, 0, 0, 1)
            dve.wait_ge(bn_ready, 1 + 2 * GROUP)
            aggregate(1, range(GROUP))
            inverse(0, 0, 0)
            inverse(0, 0, 1)
            normalise(0, 0, 0, 0)
            zT_low(0, 3, first=1)
            normalise(0, 0, 0, 1)

            def query_part(half, j):
                c = slice(half * HALF, (half + 1) * HALF)
                if j == 0 and half == 0:
                    dve.wait_ge(x_std_ready, 2)
                    nc.vector.reciprocal(x_r[:, :], x_std[:, :]).then_inc(x_stat, 1)
                    dve.wait_ge(x_stat, 3)
                    nc.vector.tensor_scalar(xq[:, :], xs[:, :], x_mv[:, 0:1], x_r[:, 1:2],
                                            ALU.subtract, ALU.mult).then_inc(xq_ready, 1)
                elif j == 3:
                    dve.wait_ge(q_sq_ready, half + 1)
                    nc.vector.tensor_reduce(q_n2[:, half, :], q_sq[:, c].rearrange("p (h d) -> p h d", d=XD), AX_X,
                                            ALU.add).then_inc(q_n2_ready, 1)
                elif j == 4:
                    dve.wait_ge(q_nrm_ready, half + 1)
                    nc.vector.reciprocal(q_rinv[:, half, :], q_nrm[:, half, :]).then_inc(q_step, 1)
                    dve.wait_ge(q_step, half + 1)
                    nc.vector.scalar_tensor_tensor(
                        qn[:, c].rearrange("p (h d) -> p h d", d=XD),
                        q_rinv[:, half, :].unsqueeze(2).broadcast_to([TOK, XH // 2, XD]), 1.0 / TINY,
                        misc[0:TOK, :].rearrange("p (h d) -> p h d", d=XD), ALU.min, ALU.mult).then_inc(qn_ready, 1)

            def weight_extra(j):
                if j == 6:
                    dve.wait_ge(bias_ps, 1)
                    nc.vector.tensor_tensor(bias_c[:, :], misc[:, 0:2 * MC], col[:, C_B1:C_B1 + 2 * MC],
                                            ALU.add).then_inc(bias_col, 1)
                elif j == 7:
                    dve.wait_ge(biasT_ps, 1)
                    nc.vector.tensor_copy(biasT[:, :], misc[0:2 * MC, 0:P]).then_inc(biasT_ready, 1)

            def body(i, first=False, last=False):
                for j in range(BODY):
                    s = i * BODY + (1 + j)
                    slot, place = where(j + GROUP)
                    group = i * 2 + (j // GROUP + 1)
                    prepare = not (last and j >= GROUP)
                    if place == 0 and prepare:
                        rstd(slot, GROUP, group)
                    head_sums(s, (1 + j) % 2, (1 + j) % KN, 0)
                    if place == 2 and not last:
                        dve.wait_ge(bn_ready, group * GROUP + (2 * GROUP + 1))
                    head_sums(s, (1 + j) % 2, (1 + j) % KN, 1)
                    for half in range(2):
                        inverse(s, (1 + j) % KN, half)
                        if place < 2 and not last:
                            if place == 0 and half == 0:
                                dve.wait_ge(ctx_in[1 - slot], i * 16 + 32)
                            stats(1 - slot, range(2 * place + half, 2 * place + half + 1))
                        if place == 2 and not last:
                            aggregate(1 - slot, range(half, half + 1))
                        if place == 3 and half == 0 and not last:
                            aggregate(1 - slot, range(2, GROUP))
                        normalise(s, (1 + j) % 2, (1 + j) % KN, half)
                    if first:
                        query_part(0, j)
                    if last:
                        query_part(1, j)
                        weight_extra(j)

            body(0, first=True)
            with dve.Fori(1, ITERS - 1) as i:
                body(i)
            body(ITERS - 1, last=True)

            def layernorm(n, src):
                dve.wait_ge(x_ready, n + 1)
                nc.vector.bn_stats(t_bn[:, n, :], src).then_inc(tbn_ready, 1)
                dve.wait_ge(tbn_ready, n + 1)
                nc.vector.bn_aggr(t_mv[:, n, :], t_bn[:, n, :]).then_inc(tmv_ready, 1)
                dve.wait_ge(tmv_ready, n + 1)
                if n == 2:
                    nc.vector.tensor_scalar(t_ve[:, n, 1:2], t_mv[:, n, 1:2], 1.0 + EPS, EPS * EPS,
                                            ALU.mult, ALU.add).then_inc(ve_ready, 1)
                nc.vector.tensor_scalar(t_ve[:, n, 0:1], t_mv[:, n, 1:2], EPS, None, ALU.add).then_inc(ve_ready, 1)
                dve.wait_ge(tr_ready, n + 1)
                which = 1 if n == 2 else 0
                nc.vector.tensor_scalar(t_hat[:, n, :], src, t_mv[:, n, 0:1], t_r[:, n, which:which + 1],
                                        ALU.subtract, ALU.mult).then_inc(hat_ready, 1)

            dve.wait_ge(g_added, TILES + 1)
            nc.vector.tensor_copy(gT[:, HALF:INNER], ps[:, 1, :]).then_inc(gT_hi_ready, 1)
            dve.wait_ge(zero_ready, 1)
            for half in range(2):
                dve.wait_ge(m_ready, half + 1)
                nc.vector.tensor_copy(m_bd[XD:P, 4 * half:4 * half + 4, XD:P],
                                      ps[XD:P, 2 + half, :].rearrange("p (c n) -> p c n", n=P)[:, :, XD:P]
                                      ).then_inc(mbd_hi_ready, 1)
            dve.wait_ge(oT_ps, 2)
            nc.vector.tensor_copy(oT[:, PAIRS // 2:PAIRS, :], ps[:, 5, 0:256].rearrange("p (c t) -> p c t", t=TOK)
                                  ).then_inc(oT_hi_ready, 1)
            dve.wait_ge(y1_ready, 1)
            dve.wait_ge(res_ready, 3)
            nc.vector.tensor_tensor(x1[:, :], ps[0:TOK, 6, 0:D], xl_bo[:, :], ALU.add).then_inc(x_ready, 1)
            layernorm(0, x1[:, :])
            nc.vector.tensor_tensor(x1_r[:, :], x1[:, :], x_b2[:, :], ALU.add).then_inc(rest_ready, 1)
            dve.wait_ge(hatT_ps, 1)
            nc.vector.tensor_copy(hatT[:, 0, 0:TOK], ps[:, 6, 0:TOK]).then_inc(hatT_ready, 1)
            dve.wait_ge(y2_ready, 1)
            dve.wait_ge(rest_ready, 1)
            nc.vector.tensor_tensor(x2[:, :], ps[0:TOK, 0, 0:D], x1_r[:, :], ALU.add).then_inc(x_ready, 1)
            layernorm(1, x2[:, :])
            nc.vector.tensor_tensor(x2_r[:, :], x2[:, :], row[0:TOK, R_ABO:R_ABO + D], ALU.add).then_inc(rest_ready, 1)
            dve.wait_ge(hatT_ps, 2)
            nc.vector.tensor_copy(hatT[:, 1, :].rearrange("p (a t) -> p a t", a=2),
                                  ps[:, 6, 0:TOK].unsqueeze(1).broadcast_to([P, 2, TOK])).then_inc(hatT_ready, 1)
            dve.wait_ge(qkv_ps, 1)
            nc.vector.scalar_tensor_tensor(
                q_heads[:, :, :], ps[:, 7, 0:TOK].unsqueeze(1).broadcast_to([P, ROWG, TOK]), col[:, 6:7],
                cst[:, C_HEAD:C_HEAD + ROWG].unsqueeze(2).broadcast_to([P, ROWG, TOK]),
                ALU.add, ALU.mult).then_inc(qk_ready, 1)
            dve.wait_ge(qkv_ps, 2)
            nc.vector.scalar_tensor_tensor(
                k_groups[:, :, :], ps[:, 5, 0:TOK].unsqueeze(1).broadcast_to([P, ROWG, TOK]), col[:, 7:8],
                cst[:, C_GRP:C_GRP + ROWG].unsqueeze(2).broadcast_to([P, ROWG, TOK]),
                ALU.add, ALU.mult).then_inc(qk_ready, 1)
            for g in range(2):
                dve.wait_ge(s_ps, g + 1)
                nc.vector.tensor_tensor(scores[:, 4 * g:4 * g + 4, :],
                                        ps[:, 2 + g, 0:4 * TOK].rearrange("p (c t) -> p c t", t=TOK),
                                        cst[:, C_CAUSAL:C_CAUSAL + TOK].unsqueeze(1).broadcast_to([P, 4, TOK]),
                                        ALU.mult).then_inc(s_ready, 1)
            dve.wait_ge(decay_ready, 1)
            for g in range(2):
                dve.wait_ge(ao_ps, g + 1)
                nc.vector.tensor_tensor(a_heads[:, 4 * g:4 * g + 4, :],
                                        ps[:, 2 + g, 0:4 * TOK].rearrange("p (c t) -> p c t", t=TOK),
                                        decay_heads[:, 4 * g:4 * g + 4, :], ALU.mult).then_inc(ao_ready, 1)
            dve.wait_ge(ao_ready, 2)
            nc.vector.tensor_reduce(a_outT[:, :], a_heads[:, :, :].rearrange("p c t -> p t c"), AX_X,
                                    ALU.add).then_inc(aoT_ready, 1)
            dve.wait_ge(y3_ready, 1)
            dve.wait_ge(rest_ready, 2)
            nc.vector.tensor_tensor(x3[:, :], ps[0:TOK, 0, 0:D], x2_r[:, :], ALU.add).then_inc(x_ready, 1)
            layernorm(2, x3[:, :])
            dve.wait_ge(tr_ready, 4)
            nc.vector.tensor_scalar(u[:, :], x3[:, :], t_mv[:, 2, 0:1], t_r[:, 2, 0:1],
                                    ALU.subtract, ALU.mult).then_inc(u_ready, 1)
            dve.wait_ge(hatT_ps, 3)
            nc.vector.tensor_copy(hatT[:, 2, 0:TOK], ps[:, 6, 0:TOK]).then_inc(hatT_ready, 1)
            dve.wait_ge(u_ready, 1)
            nc.vector.tensor_tensor(x3_u[:, :], x3[:, :], u[:, :], ALU.add).then_inc(u_ready, 1)
            dve.wait_ge(u_ready, 2)
            nc.vector.tensor_tensor(x3_r[:, :], x3_u[:, :], fb_half[:, :], ALU.add).then_inc(rest_ready, 1)
            dve.wait_ge(y4_ready, 1)
            dve.wait_ge(rest_ready, 3)
            nc.vector.scalar_tensor_tensor(y_out[:, :], ps[0:TOK, 1, 0:D], 0.5, x3_r[:, :],
                                           ALU.mult, ALU.add).then_inc(final_ready, 1)

        @block.tensor
        def _(pe):
            mm = nc.tensor.matmul

            def transposes(slot, tiles, first=0, end=GROUP, bank=6):
                pe.wait_ge(z_ready, tiles)
                for j in range(first, end):
                    last = nc.tensor.transpose(ps[:, bank, j * P:(j + 1) * P], z[:, slot, j, :], ident)
                last.then_inc(zT_ready, 1)

            def transposes_split(slot, halves):
                pe.wait_ge(z_lo_ready, halves)
                for part, to in ((z_hi, zT_hi_ps), (z_lo, zT_lo_ps)):
                    for j in range(GROUP):
                        last = nc.tensor.transpose(to[:, j * P:(j + 1) * P], part[:, slot, j, :], ident_r[:, :])
                last.then_inc(zT_ready, 1)

            def keys(s, buf, slot, place, set_no=None, lead=False):
                if set_no is not None:
                    pe.wait_ge(hi_ready, set_no)
                    pe.wait_ge(lo_ready, set_no)
                hi = zT_hi[:, slot, place * P:(place + 1) * P]
                lo = zT_lo[:, slot, place * P:(place + 1) * P]
                for half in range(2):
                    if lead:
                        pe.wait_ge(wk_lo_ready, half + 1)
                    if not (type(s) is int and s < 2):
                        pe.wait_ge(kn_ready, s * 2 + (half - 3))
                    c = slice(half * HALF, (half + 1) * HALF)
                    o = k_ps[buf][:, half, :]
                    mm(o, hi, wk_lo[:, c], start=True, stop=False)
                    mm(o, lo, wk_hi[:, c], start=False, stop=False)
                    mm(o, hi, wk_hi[:, c], start=False, stop=True).then_inc(k_ready, 1)

            def add_g(s, buf, slot, place, first=False, final=False, split=True):
                lower, upper = g_ps[:, 0, :], g_ps[:, 1, :]
                pe.wait_ge(kn_ready, s * 2 + 1)
                last = mm(lower, z[:, slot, place, :], kn[:, buf, 0:HALF], start=first, stop=final)
                if final:
                    last.then_inc(g_added, 1)
                if split:
                    pe.wait_ge(kn_hi_ready, s - (FIRST_SPLIT - 1))
                    mm(upper, z_lo[:, slot, place, :], kn_hi[:, buf, :], start=False, stop=False)
                    mm(upper, z_hi[:, slot, place, :], kn_hi[:, buf, :], start=False, stop=False)
                    pe.wait_ge(kn_lo_ready, s - (FIRST_SPLIT - 1))
                    last = mm(upper, z_hi[:, slot, place, :], kn_lo[:, buf, :], start=False, stop=False)
                else:
                    pe.wait_ge(kn_ready, s * 2 + 2)
                    last = mm(upper, z[:, slot, place, :], kn[:, buf, HALF:INNER], start=first, stop=final)
                last.then_inc(g_added, 1)

            def keep_clock(bank, products):
                for _ in range(products):
                    mm(ps[:, bank, :], zeros[:, 0:P], zeros[:, :], start=True, stop=True)

            pe.wait_ge(eps_ready, 3)
            keep_clock(7, WARM)
            pe.wait_ge(fold_ready, 3)
            for half in range(2):
                pe.wait_ge(in_wk[half], 16)
                mm(k_ps[0][:, half, :], fold[:, :], wk_s[:, half * HALF:(half + 1) * HALF], start=True,
                   stop=True).then_inc(wkf_ready, 1)
            transposes(2, 1, end=1)
            transposes(0, 2, end=1, bank=7)
            keys(0, 0, 2, 0, set_no=1, lead=True)

            def query_part(half, j):
                if j == 0 and half == 0:
                    keep_clock(0, 9)
                elif j == 3:
                    pe.wait_ge(xqT_ready, 1)
                    pe.wait_ge(in_wq, 16)
                    pe.wait_ge(lo_ready, 4 if half == 0 else 2 * ITERS + 2)
                    mm(misc[0:TOK, :], xqT[:, :], wq_s[:, half * HALF:(half + 1) * HALF], start=True,
                       stop=True).then_inc(q_ready, 1)

            def weight_extra(j):
                if j in (0, 1):
                    if j == 0:
                        pe.wait_ge(in_wv, 16)
                        pe.wait_ge(lo_ready, 2 * ITERS + 1)
                    else:
                        pe.wait_ge(wv_ready, 1)
                    mm(misc, fold[:, :], wv_s[:, j * HALF:(j + 1) * HALF], start=True, stop=True).then_inc(wvf_ready, 1)
                elif j == 5:
                    pe.wait_ge(qn_ready, 2)
                    for c in range(PAIRS):
                        last = nc.tensor.transpose(misc[:, c * TOK:(c + 1) * TOK], qn[:, c * P:(c + 1) * P],
                                                   ident[0:TOK, 0:TOK])
                    last.then_inc(qnT_ps, 1)
                elif j == 6:
                    pe.wait_ge(in_pool_w, 48)
                    pe.wait_ge(fc1_ready, 1)
                    pe.wait_ge(qnT_ready, 1)
                    for c in range(MC):
                        mm(misc[:, c:c + 1], w1_s[:, c * P:(c + 1) * P], col[:, 3:4], start=True, stop=True)
                    for c in range(MC):
                        last = mm(misc[:, MC + c:MC + c + 1], fc1_d[:, c * P:(c + 1) * P], col[:, 5:6], start=True, stop=True)
                    last.then_inc(bias_ps, 1)
                elif j == 7:
                    pe.wait_ge(bias_col, 1)
                    nc.tensor.transpose(misc[0:2 * MC, 0:P], bias_c[:, :], ident).then_inc(biasT_ps, 1)

            def body(i, first=False, last=False):
                for j in range(BODY):
                    s = i * BODY + (1 + j)
                    slot, place = where(j)
                    group = i * 2 + j // GROUP
                    if place == 3 and not (last and j >= GROUP):
                        if first:
                            pe.wait_ge(ident_ready, 1)
                            if j < GROUP:
                                pe.wait_ge(xqT_ready, 1)
                            else:
                                pe.wait_ge(qn_ready, 1)
                        if last:
                            pe.wait_ge(wv_ready, 2)
                        transposes_split(where(j + GROUP)[0], group * 2 + 2)
                    if first and j < 2:
                        keys(s, (1 + j) % 2, slot, place, set_no=2 + j)
                    else:
                        keys(s, (1 + j) % 2, slot, place, set_no=group + 3 if place == 0 else None)
                    if first and j == 0:
                        transposes(0, 1 + GROUP, first=1)
                    if first and j == 2:
                        pe.wait_ge(xq_ready, 1)
                        nc.tensor.transpose(misc[:, 0:TOK], xq[:, :], ident[0:TOK, 0:TOK]).then_inc(xqT_ps, 1)
                    if first and j < 2:
                        if j == 1:
                            add_g(0, 0, 2, 0, first=True, split=False)
                    else:
                        add_g(s - 2, (j - 1) % KN, *where((j - 2) % BODY), split=not first or j - 1 >= FIRST_SPLIT)
                    if first:
                        query_part(0, j)
                    if last:
                        query_part(1, j)
                        weight_extra(j)

            body(0, first=True)
            with pe.Fori(1, ITERS - 1) as i:
                body(i)
            body(ITERS - 1, last=True)
            add_g(TILES - 2, (TILES - 2) % KN, *where(BODY - 2))
            add_g(TILES - 1, (TILES - 1) % KN, *where(BODY - 1), final=True, split=False)

            for half in range(2):
                if half == 0:
                    pe.wait_ge(gT_ready, 1)
                    pe.wait_ge(wv_ready, 2)
                else:
                    pe.wait_ge(gT_hi_ready, 1)
                for c in range(4 * half, 4 * half + 4):
                    last = mm(ps[:, 2 + half, (c % 4) * P:(c % 4 + 1) * P], gT[:, c * P:(c + 1) * P],
                              wv_f[:, c * P:(c + 1) * P], start=True, stop=True)
                last.then_inc(m_ready, 1)
            for half in range(2):
                pe.wait_ge(mbd_lo_ready, half + 1)
                pe.wait_ge(mbd_hi_ready, half + 1)
                for c in range(4 * half, 4 * half + 4):
                    last = mm(ps[:, 4 + half, (c % 4) * TOK:(c % 4 + 1) * TOK], m_bd[:, c, :], qnT[:, c, :],
                              start=True, stop=True)
                last.then_inc(oT_ps, 1)
            pe.wait_ge(in_tail_w, 16 * 7)
            for half in range(2):
                if half == 0:
                    pe.wait_ge(oT_ready, 1)
                else:
                    pe.wait_ge(oT_hi_ready, 1)
                for c in range(4 * half, 4 * half + 4):
                    last = mm(ps[0:TOK, 6, 0:D], oT[:, c, :], wo_s[:, c, :], start=(c == 0), stop=(c == PAIRS - 1))
            last.then_inc(y1_ready, 1)

            def hat_transpose(n):
                pe.wait_ge(hat_ready, n + 1)
                nc.tensor.transpose(ps[:, 6, 0:TOK], t_hat[:, n, :], ident[0:TOK, 0:TOK]).then_inc(hatT_ps, 1)

            def hidden_bias(n):
                pe.wait_ge(biasT_ready, 1)
                mm(ps[:, 7, 0:MC * TOK], biasT[:, :], sel[:, n * MC * TOK:(n + 1) * MC * TOK], start=True, stop=False,
                   skip_group_check=True)

            hidden_bias(0)
            keep_clock(4, 7)
            hat_transpose(0)
            pe.wait_ge(hatT_ready, 1)
            for c in range(MC):
                last = mm(ps[:, 7, c * TOK:(c + 1) * TOK], w1_g[:, c * P:(c + 1) * P], hatT[:, 0, 0:TOK],
                          start=False, stop=(c == MC - 1), skip_group_check=True)
            last.then_inc(h1_ps, 1)
            keep_clock(4, 2)
            pe.wait_ge(h1_ready, 1)
            for c in range(MC):
                last = mm(ps[0:TOK, 0, 0:D], h1[:, c * TOK:(c + 1) * TOK], w2_s[:, c, :], start=(c == 0), stop=(c == MC - 1))
            last.then_inc(y2_ready, 1)
            keep_clock(4, 9)
            hat_transpose(1)
            pe.wait_ge(hatT_ready, 2)
            mm(ps[:, 7, 0:TOK], attn_w[:, 0, :], hatT[:, 1, 0:TOK], start=True, stop=True).then_inc(qkv_ps, 1)
            mm(ps[:, 5, 0:TOK], attn_w[:, 1, :], hatT[:, 1, 0:TOK], start=True, stop=True).then_inc(qkv_ps, 1)
            pe.wait_ge(in_row, 16)
            pe.wait_ge(zero_ready, 3)
            mm(ps[:, 1, 256:384], hatT[:, 1, :], attn_w[:, 2, :], start=True, stop=False)
            mm(ps[:, 1, 256:384], ones_row[0:1, :], row[0:1, R_BV:R_BV + D], start=False, stop=True).then_inc(qkv_ps, 1)
            pe.wait_ge(qk_ready, 2)
            for g in range(2):
                mm(ps[:, 2 + g, 0:4 * TOK], k_groups[:, 2 * g:2 * g + 2, :], q_heads[:, :, :],
                   start=True, stop=True).then_inc(s_ps, 1)
            keep_clock(4, 1)
            pe.wait_ge(v_ready, 2)
            for g in range(2):
                pe.wait_ge(s_ready, g + 1)
                mm(ps[:, 2 + g, 0:4 * TOK], v_bd[:, :], scores[:, 4 * g:4 * g + 4, :], start=True,
                   stop=True).then_inc(ao_ps, 1)
            hidden_bias(1)
            keep_clock(4, 4)
            pe.wait_ge(aoT_ready, 1)
            mm(ps[0:TOK, 0, 0:D], a_outT[:, :], attn_w[:, 3, :], start=True, stop=True).then_inc(y3_ready, 1)
            keep_clock(4, 8)
            hat_transpose(2)
            pe.wait_ge(hatT_ready, 3)
            for c in range(MC):
                last = mm(ps[:, 7, c * TOK:(c + 1) * TOK], fc1_g[:, c * P:(c + 1) * P], hatT[:, 2, 0:TOK],
                          start=False, stop=(c == MC - 1), skip_group_check=True)
            last.then_inc(h2_ps, 1)
            keep_clock(4, 2)
            pe.wait_ge(h2_ready, 1)
            pe.wait_ge(fc2_ready, 1)
            for c in range(MC):
                last = mm(ps[0:TOK, 1, 0:D], h2[:, c * TOK:(c + 1) * TOK], fc2_d[:, c, :], start=(c == 0), stop=(c == MC - 1))
            last.then_inc(y4_ready, 1)


def kernel(x, ctx_1024, L0_xattn_wq, L0_xattn_wk, L0_xattn_wv, L0_xattn_wo, L0_xattn_bo, L0_xattn_w1, L0_xattn_b1,
           L0_xattn_w2, L0_xattn_b2, L0_xattn_ln1_g, L0_xattn_ln1_b, L0_xattn_ln2_g, L0_xattn_ln2_b, L0_attn_Wq,
           L0_attn_bq, L0_attn_Wk, L0_attn_bk, L0_attn_Wv, L0_attn_bv, L0_attn_Wo, L0_attn_bo, L0_attn_gamma,
           L0_ffn_ln_gamma, L0_ffn_ln_beta, L0_ffn_fc1_q, L0_ffn_fc1_scales, L0_ffn_fc1_bias, L0_ffn_fc2_q,
           L0_ffn_fc2_scales, L0_ffn_fc2_bias):
    import numpy as np
    import concourse.bacc as bacc
    from concourse import mybir as mb
    from concourse.bass_utils import run_bass_kernel_spmd

    lay = np.ascontiguousarray
    chunks = lambda v: np.asarray(v).reshape(MC, P).T
    column = lambda v: np.asarray(v).reshape(P, 1)
    cols = np.concatenate([column(v) for v in (L0_xattn_ln1_g, L0_xattn_ln1_b, L0_xattn_ln2_g, L0_xattn_ln2_b,
                                               L0_ffn_ln_gamma, L0_ffn_ln_beta, L0_attn_bq, L0_attn_bk)]
                          + [chunks(L0_xattn_b1), chunks(L0_ffn_fc1_bias),
                             column(np.repeat(np.asarray(L0_attn_gamma), AD))], axis=1)
    rows = np.concatenate([np.asarray(v).reshape(-1) for v in (
        L0_xattn_bo, L0_xattn_b2, L0_attn_bo, L0_ffn_fc2_bias, L0_attn_bv, L0_ffn_fc1_scales,
        L0_ffn_fc2_scales)])
    p = np.arange(P)
    consts = np.zeros((P, CCW), np.float32)
    consts[:, C_ID:C_ID + P] = np.eye(P)
    consts[:, C_CAUSAL:C_CAUSAL + TOK] = (p[:, None] % TOK) <= np.arange(TOK)[None, :]
    consts[:, C_HEAD:C_HEAD + ROWG] = (p[:, None] % (ROWG * AD)) // AD == np.arange(ROWG)[None, :]
    consts[:, C_GRP:C_GRP + ROWG] = p[:, None] // (ROWG * AD) == np.array([0, 2, 1, 3])[None, :]
    consts[:, C_H8:C_H8 + 8] = (p[:, None] % (8 * AD)) // AD == np.arange(8)[None, :]
    chunk_select = np.repeat(np.eye(2 * MC, dtype=np.float32), TOK, axis=1)

    arrays = {
        "x": lay(x[0]), "ctx": lay(ctx_1024[0]), "wq": lay(L0_xattn_wq), "wk": lay(L0_xattn_wk), "wv": lay(L0_xattn_wv),
        "wo": lay(L0_xattn_wo), "w1": lay(L0_xattn_w1), "w2": lay(L0_xattn_w2), "wqT": lay(np.asarray(L0_attn_Wq).T),
        "wkT": lay(np.asarray(L0_attn_Wk).T), "wvT": lay(np.asarray(L0_attn_Wv).T), "woT": lay(np.asarray(L0_attn_Wo).T),
        "fc1": lay(L0_ffn_fc1_q), "fc2": lay(L0_ffn_fc2_q), "cols_consts": lay(np.concatenate([consts, cols], axis=1)), "rows": lay(rows),
        "chunk_select": chunk_select,
    }
    nc = bacc.Bacc("TRN2", target_bir_lowering=False, num_devices=1)
    feeds, args = {}, []
    for name, a in arrays.items():
        feeds[f"in_{name}"] = a
        args.append(nc.dram_tensor(f"in_{name}", a.shape, mb.dt.from_np(a.dtype), kind="ExternalInput").ap())
    result = nc.dram_tensor("result", (1, TOK, D), mb.dt.float32, kind="ExternalOutput").ap()
    build_kernel(nc, *args, result[0])
    r = run_bass_kernel_spmd(nc, [feeds], core_ids=[0])
    return r.results[0]["result"]
```
